# Optimizing a Trainium2 kernel written in Bass

```python
import numpy as np
import jax
import jax.numpy as jnp

def _softmax(x, axis=-1):
    return jax.nn.softmax(x, axis=axis)

def _gelu(x):
    return jax.nn.gelu(x, approximate=True)

def _silu(x):
    return jax.nn.silu(x)

def _sigmoid(x):
    return jax.nn.sigmoid(x)

def _layernorm(x, axis=-1, eps=1e-05):
    m = jnp.mean(x, axis=axis, keepdims=True)
    v = jnp.var(x, axis=axis, keepdims=True)
    return (x - m) / jnp.sqrt(v + eps)

def _scatter_add(tgt, idx, src, axis=0):
    return tgt.at[idx].add(src)

def _segment_sum(src, seg, n):
    return jax.ops.segment_sum(src, seg, n)
kernel_name = 'mk_adj_resnorm_d4_adj_r2_267127'

def setup_inputs(seed: int=0):
    np.random.seed(seed)
    _w = jnp.asarray

    def _rec_inputs():
        import jax
        import jax.numpy as jnp
        _gk = jax.random.key(seed)
        x = -0.0005207 + 1.001 * jax.random.normal(jax.random.fold_in(_gk, 1), (32, 256, 128), jnp.float32)
        _a = jax.random.bernoulli(jax.random.fold_in(_gk, 2), 0.0078125, (32, 256, 256))
        _a = jnp.logical_or(_a, jnp.swapaxes(_a, -1, -2))
        _a = jnp.logical_or(_a, jnp.eye(256, dtype=bool))
        _af = _a.astype(jnp.float32)
        adj = _af
        return (x, adj)
    x, adj = _rec_inputs()

    def _L0_gnn_setup():
        import jax, jax.numpy as jnp
        import numpy as np
        B, N, IN_DIM, OUT_DIM, H = (8, 512, 128, 128, 4)
        D = OUT_DIM // H
        NEG_INF = -9000000000000000.0
        LRELU_SLOPE = 0.2
        key = jax.random.key(seed)
        k1, k2, k3, k4 = jax.random.split(key, 4)
        x = jax.random.normal(k1, (B, N, IN_DIM), dtype=jnp.float32)
        adj = jax.random.randint(k2, (B, N, N), 0, 2).astype(jnp.float32)
        W = jax.random.normal(k3, (IN_DIM, H * D), dtype=jnp.float32) * jnp.sqrt(2.0 / (IN_DIM + H * D))
        a = jax.random.normal(k4, (H, 2 * D), dtype=jnp.float32) * jnp.sqrt(2.0 / (H + 2 * D))
        return {'x': x, 'adj': adj, 'W': W, 'a': a}
    _L0_gnn_all = _L0_gnn_setup()
    _L0_gnn_in = {k: v for k, v in _L0_gnn_all.items() if k in ('W', 'a')}
    del _L0_gnn_all

    def _L1_gnn_setup():
        import jax, jax.numpy as jnp
        import numpy as np
        H = 4
        NEG = -9000000000000000.0
        key = jax.random.key(seed)
        k1, k2, k3, k4 = jax.random.split(key, 4)
        B, N, D = (8, 512, 128)
        dh = D // H
        return {'node_features': jax.random.normal(k1, (B, N, D), dtype=jnp.float32), 'adjacency': jax.random.uniform(k2, (B, N, N), dtype=jnp.float32), 'W_proj': jax.random.normal(k3, (D, D), dtype=jnp.float32) * (1.0 / np.sqrt(D)), 'a_w': jax.random.normal(k4, (1, 2 * dh + 1), dtype=jnp.float32) * 0.1, 'bias': jnp.zeros((D,), dtype=jnp.float32)}
    _L1_gnn_all = _L1_gnn_setup()
    _L1_gnn_in = {k: v for k, v in _L1_gnn_all.items() if k in ('W_proj', 'a_w', 'bias')}
    del _L1_gnn_all

    def _L2_gnn_setup():
        import jax, jax.numpy as jnp
        import numpy as np
        from jax import lax
        DIM = 128
        EPS = 1e-05

        def _bn(h, g, b, m, v):
            scale = g / jnp.sqrt(v + EPS)
            return h * scale[None, :, None] + (b - m * scale)[None, :, None]

        def _conv1d(h, w, pad):
            return lax.conv_general_dilated(h, w, window_strides=(1,), padding=[(pad, pad)], dimension_numbers=('NCH', 'OIH', 'NCH'))
        key = jax.random.key(seed)
        ks = jax.random.split(key, 16)
        bs, n, d = (16, 1024, DIM)
        s = 0.05
        return {'x': jax.random.normal(ks[0], (bs, n, d), jnp.float32), 'mask': jnp.ones((bs, n, n), jnp.float32), 'w_se': jax.random.normal(ks[1], (3, d), jnp.float32) * s, 'b_se': jnp.zeros((3,), jnp.float32), 'conv1_w': jax.random.normal(ks[2], (d, d, 1), jnp.float32) * s, 'bn1_g': jnp.ones((d,), jnp.float32), 'bn1_b': jnp.zeros((d,), jnp.float32), 'bn1_m': jnp.zeros((d,), jnp.float32), 'bn1_v': jnp.ones((d,), jnp.float32), 'conv2_w': jax.random.normal(ks[3], (d, d, 17), jnp.float32) * s, 'bn2_g': jnp.ones((d,), jnp.float32), 'bn2_b': jnp.zeros((d,), jnp.float32), 'bn2_m': jnp.zeros((d,), jnp.float32), 'bn2_v': jnp.ones((d,), jnp.float32), 'w_msg': jax.random.normal(ks[4], (d, d), jnp.float32) * s, 'b_msg': jnp.zeros((d,), jnp.float32), 'w_ih': jax.random.normal(ks[5], (3 * d, 2 * d), jnp.float32) * s, 'b_ih': jnp.zeros((3 * d,), jnp.float32), 'w_hh': jax.random.normal(ks[6], (3 * d, d), jnp.float32) * s, 'b_hh': jnp.zeros((3 * d,), jnp.float32)}
    _L2_gnn_all = _L2_gnn_setup()
    _L2_gnn_in = {k: v for k, v in _L2_gnn_all.items() if k in ('w_se', 'b_se', 'conv1_w', 'bn1_g', 'bn1_b', 'bn1_m', 'bn1_v', 'conv2_w', 'bn2_g', 'bn2_b', 'bn2_m', 'bn2_v', 'w_msg', 'b_msg', 'w_ih', 'b_ih', 'w_hh', 'b_hh')}
    del _L2_gnn_all

    def _L3_gnn_setup():
        import jax, jax.numpy as jnp
        import numpy as np
        B, K, H = (32, 512, 128)
        LN_EPS = 1e-05

        def layer_norm(x, gamma, beta):
            mu = jnp.mean(x, axis=-1, keepdims=True)
            var = jnp.mean(jnp.square(x - mu), axis=-1, keepdims=True)
            return (x - mu) * jax.lax.rsqrt(var + LN_EPS) * gamma + beta
        key = jax.random.key(seed)
        k1, k2, k3, k4 = jax.random.split(key, 4)
        x = jax.random.normal(k1, (B, K, H), dtype=jnp.float32)
        adj = jax.random.uniform(k2, (B, K, K), dtype=jnp.float32)
        s = 1.0 / np.sqrt(H)
        W_rel = jax.random.normal(k3, (H, H), dtype=jnp.float32) * s
        b_rel = jnp.zeros((H,), dtype=jnp.float32)
        W_root = jax.random.normal(k4, (H, H), dtype=jnp.float32) * s
        ln_gamma = jnp.ones((H,), dtype=jnp.float32)
        ln_beta = jnp.zeros((H,), dtype=jnp.float32)
        return {'x': x, 'adj': adj, 'W_rel': W_rel, 'b_rel': b_rel, 'W_root': W_root, 'ln_gamma': ln_gamma, 'ln_beta': ln_beta}
    _L3_gnn_all = _L3_gnn_setup()
    _L3_gnn_in = {k: v for k, v in _L3_gnn_all.items() if k in ('W_rel', 'b_rel', 'W_root', 'ln_gamma', 'ln_beta')}
    del _L3_gnn_all
    return {'x': x, 'adj': adj, 'L0_gnn_W': _L0_gnn_in['W'], 'L0_gnn_a': _L0_gnn_in['a'], 'L1_gnn_W_proj': _L1_gnn_in['W_proj'], 'L1_gnn_a_w': _L1_gnn_in['a_w'], 'L1_gnn_bias': _L1_gnn_in['bias'], 'L2_gnn_w_se': _L2_gnn_in['w_se'], 'L2_gnn_b_se': _L2_gnn_in['b_se'], 'L2_gnn_conv1_w': _L2_gnn_in['conv1_w'], 'L2_gnn_bn1_g': _L2_gnn_in['bn1_g'], 'L2_gnn_bn1_b': _L2_gnn_in['bn1_b'], 'L2_gnn_bn1_m': _L2_gnn_in['bn1_m'], 'L2_gnn_bn1_v': _L2_gnn_in['bn1_v'], 'L2_gnn_conv2_w': _L2_gnn_in['conv2_w'], 'L2_gnn_bn2_g': _L2_gnn_in['bn2_g'], 'L2_gnn_bn2_b': _L2_gnn_in['bn2_b'], 'L2_gnn_bn2_m': _L2_gnn_in['bn2_m'], 'L2_gnn_bn2_v': _L2_gnn_in['bn2_v'], 'L2_gnn_w_msg': _L2_gnn_in['w_msg'], 'L2_gnn_b_msg': _L2_gnn_in['b_msg'], 'L2_gnn_w_ih': _L2_gnn_in['w_ih'], 'L2_gnn_b_ih': _L2_gnn_in['b_ih'], 'L2_gnn_w_hh': _L2_gnn_in['w_hh'], 'L2_gnn_b_hh': _L2_gnn_in['b_hh'], 'L3_gnn_W_rel': _L3_gnn_in['W_rel'], 'L3_gnn_b_rel': _L3_gnn_in['b_rel'], 'L3_gnn_W_root': _L3_gnn_in['W_root'], 'L3_gnn_ln_gamma': _L3_gnn_in['ln_gamma'], 'L3_gnn_ln_beta': _L3_gnn_in['ln_beta']}

def reference(x, adj, L0_gnn_W, L0_gnn_a, L1_gnn_W_proj, L1_gnn_a_w, L1_gnn_bias, L2_gnn_w_se, L2_gnn_b_se, L2_gnn_conv1_w, L2_gnn_bn1_g, L2_gnn_bn1_b, L2_gnn_bn1_m, L2_gnn_bn1_v, L2_gnn_conv2_w, L2_gnn_bn2_g, L2_gnn_bn2_b, L2_gnn_bn2_m, L2_gnn_bn2_v, L2_gnn_w_msg, L2_gnn_b_msg, L2_gnn_w_ih, L2_gnn_b_ih, L2_gnn_w_hh, L2_gnn_b_hh, L3_gnn_W_rel, L3_gnn_b_rel, L3_gnn_W_root, L3_gnn_ln_gamma, L3_gnn_ln_beta):
    import jax
    import jax.numpy as jnp

    def _L0_gnn_ref(x, adj, W, a):
        import jax, jax.numpy as jnp
        import numpy as np
        B, N, IN_DIM, OUT_DIM, H = (8, 512, 128, 128, 4)
        D = OUT_DIM // H
        NEG_INF = -9000000000000000.0
        LRELU_SLOPE = 0.2
        h = jnp.einsum('bni,io->bno', x, W).reshape(x.shape[0], x.shape[1], H, D)
        h = h.transpose(0, 2, 1, 3)
        a1, a2 = (a[:, :D], a[:, D:])
        e_i = jnp.einsum('bhnd,hd->bhn', h, a1)
        e_j = jnp.einsum('bhmd,hd->bhm', h, a2)
        e = e_i[:, :, :, None] + e_j[:, :, None, :]
        e = jnp.where(e > 0, e, LRELU_SLOPE * e)
        e = jnp.where(adj[:, None, :, :] > 0, e, NEG_INF)
        attn = jax.nn.softmax(e, axis=-1)
        out = jnp.einsum('bhnm,bhmd->bhnd', attn, h)
        out = out.transpose(0, 2, 1, 3).reshape(x.shape[0], x.shape[1], H * D)
        return out

    def _L1_gnn_ref(node_features, adjacency, W_proj, a_w, bias):
        import jax, jax.numpy as jnp
        import numpy as np
        H = 4
        NEG = -9000000000000000.0
        B, N, D = node_features.shape
        dh = D // H
        h = (node_features @ W_proj.T).reshape(B, N, H, dh)
        w = a_w[0]
        wl, wr, we = (w[:dh], w[dh:2 * dh], w[2 * dh])
        s_left = jnp.einsum('bihd,d->bih', h, wl)
        s_right = jnp.einsum('bjhd,d->bjh', h, wr)
        scores = s_left[:, :, None, :] + s_right[:, None, :, :] + adjacency[..., None] * we
        scores = jax.nn.leaky_relu(scores, negative_slope=0.2)
        pad = (adjacency <= 1e-05).astype(scores.dtype)
        scores = scores + (NEG * pad)[..., None]
        attn = jax.nn.softmax(scores, axis=2)
        agg = jnp.einsum('bijh,bjhd->bihd', attn, h).reshape(B, N, D)
        out = jax.nn.leaky_relu(node_features + agg + bias, negative_slope=0.5)
        return out

    def _L2_gnn_ref(x, mask, w_se, b_se, conv1_w, bn1_g, bn1_b, bn1_m, bn1_v, conv2_w, bn2_g, bn2_b, bn2_m, bn2_v, w_msg, b_msg, w_ih, b_ih, w_hh, b_hh):
        import jax, jax.numpy as jnp
        import numpy as np
        from jax import lax
        DIM = 128
        EPS = 1e-05

        def _bn(h, g, b, m, v):
            scale = g / jnp.sqrt(v + EPS)
            return h * scale[None, :, None] + (b - m * scale)[None, :, None]

        def _conv1d(h, w, pad):
            return lax.conv_general_dilated(h, w, window_strides=(1,), padding=[(pad, pad)], dimension_numbers=('NCH', 'OIH', 'NCH'))
        d = x.shape[-1]
        xc = jnp.transpose(x, (0, 2, 1))
        h = _bn(_conv1d(xc, conv1_w, 0), bn1_g, bn1_b, bn1_m, bn1_v)
        h = jax.nn.relu(h)
        h = _bn(_conv1d(h, conv2_w, 8), bn2_g, bn2_b, bn2_m, bn2_v)
        x_conv = jnp.transpose(jax.nn.relu(h + xc), (0, 2, 1))
        s = x @ w_se.T + b_se
        sq = jnp.sum(s * s, axis=-1)
        dist = sq[:, :, None] + sq[:, None, :] - 2.0 * jnp.einsum('bnd,bmd->bnm', s, s)
        A = jnp.exp(-dist) * mask
        msg = jax.nn.relu(x @ w_msg.T + b_msg)
        x_nmp = jnp.einsum('bnm,bmd->bnd', A, msg)
        x_in = jnp.concatenate([x_conv, x_nmp], axis=-1)
        gi = x_in @ w_ih.T + b_ih
        gh = x @ w_hh.T + b_hh
        gi_r, gi_z, gi_n = (gi[..., :d], gi[..., d:2 * d], gi[..., 2 * d:])
        gh_r, gh_z, gh_n = (gh[..., :d], gh[..., d:2 * d], gh[..., 2 * d:])
        r = jax.nn.sigmoid(gi_r + gh_r)
        z = jax.nn.sigmoid(gi_z + gh_z)
        nn_ = jnp.tanh(gi_n + r * gh_n)
        return (1.0 - z) * nn_ + z * x

    def _L3_gnn_ref(x, adj, W_rel, b_rel, W_root, ln_gamma, ln_beta):
        import jax, jax.numpy as jnp
        import numpy as np
        B, K, H = (32, 512, 128)
        LN_EPS = 1e-05

        def layer_norm(x, gamma, beta):
            mu = jnp.mean(x, axis=-1, keepdims=True)
            var = jnp.mean(jnp.square(x - mu), axis=-1, keepdims=True)
            return (x - mu) * jax.lax.rsqrt(var + LN_EPS) * gamma + beta
        h = layer_norm(x, ln_gamma, ln_beta)
        agg = jnp.einsum('bij,bjh->bih', adj, h)
        conv = jnp.einsum('bkh,ho->bko', agg, W_rel) + b_rel + jnp.einsum('bkh,ho->bko', h, W_root)
        return x + jax.nn.relu(conv)
    x = _layernorm(x + _L0_gnn_ref(x, adj, L0_gnn_W, L0_gnn_a), axis=-1)
    x = _layernorm(x + _L1_gnn_ref(x, adj, L1_gnn_W_proj, L1_gnn_a_w, L1_gnn_bias), axis=-1)
    x = _layernorm(x + _L2_gnn_ref(x, adj, L2_gnn_w_se, L2_gnn_b_se, L2_gnn_conv1_w, L2_gnn_bn1_g, L2_gnn_bn1_b, L2_gnn_bn1_m, L2_gnn_bn1_v, L2_gnn_conv2_w, L2_gnn_bn2_g, L2_gnn_bn2_b, L2_gnn_bn2_m, L2_gnn_bn2_v, L2_gnn_w_msg, L2_gnn_b_msg, L2_gnn_w_ih, L2_gnn_b_ih, L2_gnn_w_hh, L2_gnn_b_hh), axis=-1)
    x = _layernorm(x + _L3_gnn_ref(x, adj, L3_gnn_W_rel, L3_gnn_b_rel, L3_gnn_W_root, L3_gnn_ln_gamma, L3_gnn_ln_beta), axis=-1)
    return x

_drawn_inputs = setup_inputs


def setup_inputs(seed=0):
    import zlib

    import numpy as np

    out = dict(_drawn_inputs(seed))
    spreads = {'L1_gnn_bias': (0.0, 0.1),
     'L2_gnn_b_se': (0.0, 0.8),
     'L2_gnn_bn1_g': (1.0, 0.6),
     'L2_gnn_bn1_b': (0.0, 0.481),
     'L2_gnn_bn1_m': (0.0, 0.399),
     'L2_gnn_bn1_v': (1.0, 0.6),
     'L2_gnn_bn2_g': (1.0, 0.56),
     'L2_gnn_bn2_b': (0.0, 0.674),
     'L2_gnn_bn2_m': (0.0, 0.653),
     'L2_gnn_bn2_v': (1.0, 0.6),
     'L2_gnn_b_msg': (0.0, 0.283),
     'L2_gnn_b_ih': (0.0, 0.1),
     'L2_gnn_b_hh': (0.0, 0.387),
     'L3_gnn_b_rel': (0.0, 0.386),
     'L3_gnn_ln_gamma': (1.0, 0.2),
     'L3_gnn_ln_beta': (0.0, 0.1)}
    factors = {}
    for name, (base, spread) in spreads.items():
        noise = np.random.default_rng([zlib.crc32(name.encode()), seed]).standard_normal(out[name].shape)
        drawn = base * np.exp(spread * noise) if base else spread * noise
        out[name] = jnp.asarray(drawn.astype(out[name].dtype))
    for name, factor in factors.items():
        out[name] = (out[name] * factor).astype(out[name].dtype)
    return out
```

```python
from contextlib import ExitStack

import numpy as np

import concourse.bass as bass
from concourse import mybir
from concourse.alu_op_type import AluOpType as ALU

F32 = mybir.dt.float32
ACT = mybir.ActivationFunctionType
AX = mybir.AxisListType

P = 128
HEADS = 4
DH = P // HEADS
NEG = -float(2 ** 53)
SLOPE = 0.2
EPS = 1e-5
TAPS = 17
PAD = TAPS // 2
LAYERS = 4

COLUMNS = [
    ("ident", P), ("w0", P), ("w1", P), ("a0l", P), ("a0r", P), ("a1l", P), ("a1r", P), ("bias1", P),
    ("conv1", P), ("conv2", TAPS * P), ("wmsg", P), ("bmsg", P), ("wse", 96),
    ("wih", 6 * P), ("whh", 3 * P), ("wrel", P), ("wroot", P), ("brel", P), ("gamma", P), ("beta", P),
    ("bn1", 4), ("bn2", 4), ("bih", 3), ("bhh", 3), ("bse", 1), ("we", 1),
]
OFFSET, WIDTH = {}, 0
for _name, _n in COLUMNS:
    OFFSET[_name] = (WIDTH, _n)
    WIDTH += _n


def build(nc, x, adj, consts, out):
    B, N, D = x.shape
    NT = N // P
    HN = HEADS * N
    STEPS = B + LAYERS - 1

    x_d = x.rearrange("b (t p) d -> b p t d", p=P)
    adj_d = adj.rearrange("b (t p) m -> b p t m", p=P)
    out_d = out.rearrange("b (t p) d -> b p t d", p=P)

    with ExitStack() as ctx:
        def sb(name, shape):
            return ctx.enter_context(nc.sbuf_tensor(name, shape, F32))

        def bank(name):
            return ctx.enter_context(nc.psum_tensor("bank_" + name, [P, 512], F32))

        cst = sb("cst", [P, WIDTH])

        def c(name, a=0, b=None):
            at, n = OFFSET[name]
            return cst[:, at + a:at + (n if b is None else b)]

        ident = c("ident")
        x_in = [[sb(f"x{s}_{p}", [P, NT, D]) for p in range(2)] for s in range(LAYERS)]
        adj_a = [sb(f"adj_a{p}", [P, NT, N]) for p in range(2)]
        adj_b = [sb(f"adj_b{p}", [P, NT, N]) for p in range(2)]
        adjT = [sb(f"adjT{p}", [P, NT, N]) for p in range(2)]
        y_out = [sb(f"y_out{p}", [P, NT, D]) for p in range(2)]
        edge0 = sb("edge0", [P, NT, N])
        edge1 = [sb(f"edge1_{p}", [P, NT, N]) for p in range(2)]
        padmask = sb("padmask", [P, NT, N])

        w_ext = [sb(f"w_ext{a}", [P, P + 2 * HEADS]) for a in range(2)]
        prod = sb("prod", [P, 4, P])
        xT01 = sb("xT01", [P, 2, N])
        he = [sb(f"he{a}", [P, NT, P + 2 * HEADS]) for a in range(2)]
        sc = [sb(f"sc{a}", [P, NT, HEADS, N]) for a in range(2)]
        low = [sb(f"low{a}", [P, NT, HEADS, N]) for a in range(2)]
        rmax = [sb(f"rmax{a}", [P, NT, HEADS]) for a in range(2)]
        pre = [sb(f"pre{a}", [P, NT, HEADS]) for a in range(2)]
        mrow = [sb(f"mrow{a}", [P, NT, HEADS]) for a in range(2)]
        off1 = [sb(f"off1_{a}", [P, NT, HEADS]) for a in range(2)]
        off2 = [sb(f"off2_{a}", [P, NT, HEADS]) for a in range(2)]
        pT = [sb(f"pT{a}", [P, NT, HEADS, N]) for a in range(2)]
        ones = sb("ones", [P, DH])
        aggT = [sb(f"aggT{a}", [P, 2, N]) for a in range(2)]
        rden = [sb(f"rden{a}", [P, NT, HEADS]) for a in range(2)]
        att = [sb(f"att{a}", [P, NT, D]) for a in range(2)]
        xb1 = sb("xb1", [P, NT, D])
        y1a = sb("y1a", [P, NT, D])
        y1b = sb("y1b", [P, NT, D])
        y = [sb(f"y{s}", [P, NT, D]) for s in range(5)]
        st = [sb(f"st{s}", [P, NT, 6]) for s in range(5)]
        mv = [sb(f"mv{s}", [P, NT, 2]) for s in range(5)]
        ve = [sb(f"ve{s}", [P, NT]) for s in range(5)]
        rstd = [sb(f"rstd{s}", [P, NT]) for s in range(5)]
        mhalf = sb("mhalf", [P, NT])
        eps = sb("eps", [P, NT])

        xT2 = sb("xT2", [P, N])
        h1 = sb("h1", [P, N + 2 * PAD])
        seL = sb("seL", [96, N])
        seR = sb("seR", [96, N])
        bse2 = sb("bse2", [P, 1])
        msg_b = sb("msg_b", [P, NT, D])
        msg = sb("msg", [P, NT, D])
        near = sb("near", [P, NT, N])
        aT = sb("aT", [P, NT, N])
        conv = sb("conv", [P, N])
        xconv = sb("xconv", [P, N])
        xnmp = sb("xnmp", [P, N])
        tr = sb("tr", [P, N])
        tz = sb("tz", [P, N])
        hb = sb("hb", [P, N])
        q = sb("q", [P, N])
        pn = sb("pn", [P, N])
        nn = sb("nn", [P, N])
        dl = sb("dl", [P, N])
        tzd = sb("tzd", [P, N])
        o2 = sb("o2", [P, N])
        yT2 = sb("yT2", [P, N])
        bn_v = sb("bn_v", [P, 2])
        bn_r = sb("bn_r", [P, 2])
        bn_s = sb("bn_s", [P, 2])
        bn_ms = sb("bn_ms", [P, 2])
        bn_b = sb("bn_b", [P, 2])
        brz = sb("brz", [P, 2])
        brzh = sb("brzh", [P, 2])
        bhnh = sb("bhnh", [P, 1])

        hn = sb("hn", [P, NT, D])
        hg = sb("hg", [P, NT, D])
        h3 = sb("h3", [P, NT, D])
        h3T = sb("h3T", [P, N])
        agg3 = sb("agg3", [P, N])
        cb = sb("cb", [P, NT, D])
        x2x = sb("x2x", [P, NT, D])

        bA, bB, bC, bD, bE, bF, bG, bH = (bank(n) for n in "ABCDEFGH")

        sems = {}

        def sem(name):
            if name not in sems:
                sems[name] = ctx.enter_context(nc.semaphore(name))
            return sems[name]

        def layer_of(name):
            return int(name[1])

        def runs(step, layer):
            return not isinstance(step, int) or 0 <= step - layer < B

        def counts(step):
            return ([step + 1 - l for l in range(LAYERS)], [step - l for l in range(LAYERS)],
                    [runs(step - 1, l) for l in range(LAYERS)])

        CHUNKS = [(0, 0), (1, 0), (0, 1), (1, 1)]
        EMPTIED = {
            "A": ["l0_xT_read", "l1_xT_read", "l2_seR", "l2_near_ready", "l0_agg_read", "l0_o_read", "l1_agg_read", "l1_o_read"],
            "B": ["l2_adjT_read", "l3_hT_read", "l3_agg_read", "l3_conv_read", "l2_back_read"],
            "C": ["l2_xT_read", "l2_msg_read", "l2_xnmp_read", "l2_rz_read"],
            "D": ["l0_he_read", "l0_exp_c0", "l0_exp_c2", "l1_exp_c0", "l1_exp_c2"],
            "E": ["l1_he_read", "l0_exp_c1", "l0_exp_c3", "l1_exp_c1", "l1_exp_c3"],
            "F": ["l0_max_p0", "l1_max_p0"],
            "G": ["l0_max_p1", "l1_max_p1"],
            "H": ["l2_conv2_read", "l2_inhn_read"],
        }

        def bank_free(step, name, mine):
            this, past, again = counts(step)
            uses = EMPTIED[name]
            for other in reversed(uses[:uses.index(mine)]):
                if runs(step, layer_of(other)):
                    return sem(other), this[layer_of(other)]
            for other in reversed(uses):
                if again[layer_of(other)]:
                    return sem(other), past[layer_of(other)]
            return None

        def sweep(eng_steps, eng):
            first = LAYERS
            pairs = (B - 1 - first) // 2
            for s in range(first):
                eng_steps(s, s % 2)
            with eng.Fori(0, pairs) as pair:
                eng_steps(pair * 2 + first, first % 2)
                eng_steps(pair * 2 + (first + 1), (first + 1) % 2)
            for s in range(first + 2 * pairs, STEPS):
                eng_steps(s, s % 2)

        block = ctx.enter_context(nc.Block())

        @block.sync
        def _(sp):
            sp.dma_start(cst[:], consts).then_inc(sem("consts"), 16)
            sp.dma_start(x_in[0][0][:], x_d[0]).then_inc(sem("l0_loaded"), 16)
            sp.dma_start(adj_a[0][:], adj_d[0]).then_inc(sem("l0_loaded"), 16)

            def step_of(s, par):
                this, past, again = counts(s)
                if not isinstance(s, int) or s + 1 < B:
                    sp.wait_ge(sem("consts"), 16)
                    if again[0]:
                        sp.wait_ge(sem("l0_sum"), past[0])
                    if again[0]:
                        sp.wait_ge(sem("l0_edge1"), past[0])
                    sp.wait_ge(sem("l0_loaded"), 32 * this[0])
                    sp.dma_start(x_in[0][1 - par][:], x_d[s + 1]).then_inc(sem("l0_loaded"), 16)
                    sp.dma_start(adj_a[1 - par][:], adj_d[s + 1]).then_inc(sem("l0_loaded"), 16)
                if not isinstance(s, int) or 0 <= s - 1 < B:
                    sp.wait_ge(sem("consts"), 16)
                    if again[2]:
                        sp.wait_ge(sem("l2_adjT_read"), past[2])
                    if runs(s, 2):
                        sp.wait_ge(sem("l2_loaded"), 16 * this[2])
                    sp.dma_start(adj_b[1 - par][:], adj_d[s - 1]).then_inc(sem("l2_loaded"), 16)
                if runs(s, 3):
                    sp.wait_ge(sem("consts"), 16)
                    if again[3]:
                        sp.wait_ge(sem("l3_stored"), 16 * past[3])
                    sp.wait_ge(sem("l3_out"), this[3])
                    sp.dma_start(out_d[s - 3], y_out[par][:]).then_inc(sem("l3_stored"), 16)

            sweep(step_of, sp)
            sp.wait_ge(sem("l3_stored"), 16 * B)

        @block.tensor
        def _(pe):
            pe.wait_ge(sem("consts"), 16)
            pe.wait_ge(sem("setup_v"), 1)

            def step_of(s, par):
                this, past, again = counts(s)
                on = [runs(s, l) for l in range(LAYERS)]

                def turn(dst, src, name, last=NT - 1, mark=True):
                    for t in range(NT):
                        mm = pe.transpose(dst[:, t * P:(t + 1) * P], src[:, t, :], ident)
                    mm.then_inc(sem(name), 1)

                def inputs01(a):
                    if a == 0:
                        pe.wait_ge(sem("l0_loaded"), 32 * this[0])
                    else:
                        if again[0]:
                            pe.wait_ge(sem("l0_x"), past[0])
                    free = bank_free(s, "A", "l0_xT_read")
                    if free:
                        pe.wait_ge(*free)
                    turn(bA[:, a * N:(a + 1) * N], x_in[a][par], f"l{a}_xT_full")

                def project(a):
                    dst, name = (bD, "D") if a == 0 else (bE, "E")
                    pe.wait_ge(sem(f"l{a}_xT_read"), this[a])
                    free = bank_free(s, name, f"l{a}_he_read")
                    if free:
                        pe.wait_ge(*free)
                    W = P + 2 * HEADS
                    for t in range(NT):
                        mm = pe.matmul(dst[:, t * W:(t + 1) * W], xT01[:, a, t * P:(t + 1) * P], w_ext[a][:],
                                       start=True, stop=True)
                    mm.then_inc(sem(f"l{a}_he_full"), 1)

                def spread(a):
                    pe.wait_ge(sem(f"l{a}_he_read"), this[a])
                    for hp, (dst, name) in enumerate(((bF, "F"), (bG, "G"))):
                        free = bank_free(s, name, f"l{a}_max_p{hp}")
                        if free:
                            pe.wait_ge(*free)
                        for h in range(2):
                            for t in range(NT):
                                at = P + HEADS + 2 * hp + h
                                mm = pe.transpose(dst[:, h * N + t * P:h * N + (t + 1) * P],
                                                  he[a][:, t, at:at + 1].broadcast_to([P, P]), ident)
                        mm.then_inc(sem(f"l{a}_spread_p{hp}"), 1)

                def turn_scores(a, k):
                    m, hp = CHUNKS[k]
                    dst, name = ((bD, "D"), (bE, "E"))[k % 2]
                    pe.wait_ge(sem(f"l{a}_sc_p{hp}"), this[a])
                    free = bank_free(s, name, f"l{a}_exp_c{k}")
                    if free:
                        pe.wait_ge(*free)
                    for h in range(2):
                        for t in range(NT):
                            mm = pe.transpose(dst[:, h * N + t * P:h * N + (t + 1) * P],
                                              sc[a][:, t, 2 * hp + h, m * P:(m + 1) * P], ident)
                    mm.then_inc(sem(f"l{a}_turned_c{k}"), 1)

                def aggregate(a):
                    pe.wait_ge(sem(f"l{a}_exp_c3"), this[a])
                    free = bank_free(s, "A", f"l{a}_agg_read")
                    if free:
                        pe.wait_ge(*free)
                    for part in range(2):
                        for m in range(NT):
                            for h in range(HEADS):
                                lhs = he[a][:, m, h * DH:(h + 1) * DH] if part == 0 else ones[:]
                                mm = pe.matmul(bA[h * DH:(h + 1) * DH, part * N:(part + 1) * N], lhs,
                                               pT[a][:, m, h, :], start=(m == 0), stop=(m == NT - 1),
                                               skip_group_check=True)
                    mm.then_inc(sem(f"l{a}_agg_full"), 1)

                def back01(a):
                    pe.wait_ge(sem(f"l{a}_agg_read"), this[a])
                    free = bank_free(s, "A", f"l{a}_o_read")
                    if free:
                        pe.wait_ge(*free)
                    for k in range(2):
                        for t in range(NT):
                            mm = pe.transpose(bA[:, k * N + t * P:k * N + (t + 1) * P],
                                              aggT[a][:, k, t * P:(t + 1) * P], ident)
                    mm.then_inc(sem(f"l{a}_o_full"), 1)

                def taps(k0, k1):
                    if k0 == 0:
                        pe.wait_ge(sem("l2_h1"), this[2])
                        free = bank_free(s, "H", "l2_conv2_read")
                        if free:
                            pe.wait_ge(*free)
                    for k in range(k0, k1):
                        mm = pe.matmul(bH[:, 0:N], c("conv2", k * P, (k + 1) * P), h1[:, k:k + N],
                                       start=(k == 0), stop=(k == TAPS - 1), skip_group_check=True)
                    if k1 == TAPS:
                        mm.then_inc(sem("l2_conv2_full"), 1)

                def gate(dst, g, last=None):
                    pe.matmul(dst, c("wih", g * P, (g + 1) * P), xconv[:], start=True, stop=False,
                              skip_group_check=True)
                    mm = pe.matmul(dst, c("wih", (3 + g) * P, (4 + g) * P), xnmp[:], start=False, stop=(g == 2),
                                   skip_group_check=True)
                    if g < 2:
                        mm = pe.matmul(dst, c("whh", g * P, (g + 1) * P), xT2[:], start=False, stop=True,
                                       skip_group_check=True)
                    return mm

                if on[0]:
                    inputs01(0)
                if on[1]:
                    inputs01(1)
                if on[2]:
                    pe.wait_ge(sem("l2_loaded"), 16 * this[2])
                    free = bank_free(s, "B", "l2_adjT_read")
                    if free:
                        pe.wait_ge(*free)
                    for m in range(NT):
                        for t in range(NT):
                            mm = pe.transpose(bB[:, m * N + t * P:m * N + (t + 1) * P],
                                              adj_b[par][:, t, m * P:(m + 1) * P], ident)
                    mm.then_inc(sem("l2_adjT_full"), 1)
                    if again[1]:
                        pe.wait_ge(sem("l1_x"), past[1])
                    free = bank_free(s, "C", "l2_xT_read")
                    if free:
                        pe.wait_ge(*free)
                    turn(bC, x_in[2][par], "l2_xT_full")
                if on[0]:
                    project(0)
                if on[1]:
                    project(1)
                if on[0]:
                    spread(0)
                if on[2]:
                    pe.wait_ge(sem("l2_xT_read"), this[2])
                    free = bank_free(s, "A", "l2_seR")
                    if free:
                        pe.wait_ge(*free)
                    pe.matmul(bA[:, 0:N], c("conv1"), xT2[:], start=True, stop=True)
                    pe.matmul(bA[0:96, N:2 * N], c("wse"), xT2[:], start=True, stop=True)\
                        .then_inc(sem("l2_c1s_full"), 1)
                    free = bank_free(s, "C", "l2_msg_read")
                    if free:
                        pe.wait_ge(*free)
                    for t in range(NT):
                        mm = pe.matmul(bC[:, t * P:(t + 1) * P], xT2[:, t * P:(t + 1) * P], c("wmsg"),
                                       start=True, stop=True)
                    mm.then_inc(sem("l2_msg_full"), 1)
                if on[3]:
                    pe.wait_ge(sem("l3_h"), this[3])
                    free = bank_free(s, "B", "l3_hT_read")
                    if free:
                        pe.wait_ge(*free)
                    turn(bB, h3, "l3_hT_full")
                if on[2]:
                    pe.wait_ge(sem("l2_se"), this[2])
                    pe.wait_ge(sem("l2_seR"), this[2])
                    free = bank_free(s, "A", "l2_near_ready")
                    if free:
                        pe.wait_ge(*free)
                    for t in range(NT):
                        mm = pe.matmul(bA[:, t * N:(t + 1) * N], seL[:, t * P:(t + 1) * P], seR[:],
                                       start=True, stop=True)
                    mm.then_inc(sem("l2_dist_full"), 1)
                    taps(0, 5)
                if on[3]:
                    free = bank_free(s, "B", "l3_agg_read")
                    if free:
                        pe.wait_ge(*free)
                    for m in range(NT):
                        mm = pe.matmul(bB[:, 0:N], h3[:, m, :], adjT[1 - par][:, m, :],
                                       start=(m == 0), stop=(m == NT - 1))
                    mm.then_inc(sem("l3_agg_full"), 1)
                if on[2]:
                    taps(5, 9)
                if on[1]:
                    spread(1)
                for k in range(4):
                    if on[0]:
                        turn_scores(0, k)
                    if on[2]:
                        taps(9 + 2 * k, 11 + 2 * k)
                if on[3]:
                    pe.wait_ge(sem("l3_agg_read"), this[3])
                    free = bank_free(s, "B", "l3_conv_read")
                    if free:
                        pe.wait_ge(*free)
                    for t in range(NT):
                        pe.matmul(bB[:, t * P:(t + 1) * P], agg3[:, t * P:(t + 1) * P], c("wrel"),
                                  start=True, stop=False)
                        mm = pe.matmul(bB[:, t * P:(t + 1) * P], h3T[:, t * P:(t + 1) * P], c("wroot"),
                                       start=False, stop=True)
                    mm.then_inc(sem("l3_conv_full"), 1)
                if on[2]:
                    pe.wait_ge(sem("l2_aT"), this[2])
                    free = bank_free(s, "C", "l2_xnmp_read")
                    if free:
                        pe.wait_ge(*free)
                    for m in range(NT):
                        mm = pe.matmul(bC[:, 0:N], msg[:, m, :], aT[:, m, :], start=(m == 0), stop=(m == NT - 1))
                    mm.then_inc(sem("l2_xnmp_full"), 1)
                if on[0]:
                    aggregate(0)
                if on[1]:
                    turn_scores(1, 0)
                    turn_scores(1, 1)
                if on[2]:
                    pe.wait_ge(sem("l2_xconv"), this[2])
                    pe.wait_ge(sem("l2_xnmp_read"), this[2])
                    free = bank_free(s, "C", "l2_rz_read")
                    if free:
                        pe.wait_ge(*free)
                    gate(bC[:, 0:N], 0)
                    gate(bC[:, N:2 * N], 1).then_inc(sem("l2_rz_full"), 1)
                if on[0]:
                    back01(0)
                if on[1]:
                    turn_scores(1, 2)
                    turn_scores(1, 3)
                if on[2]:
                    free = bank_free(s, "H", "l2_inhn_read")
                    if free:
                        pe.wait_ge(*free)
                    gate(bH[:, 0:N], 2)
                    pe.matmul(bH[:, N:2 * N], c("whh", 2 * P, 3 * P), xT2[:], start=True, stop=True,
                              skip_group_check=True).then_inc(sem("l2_inhn_full"), 1)
                if on[1]:
                    aggregate(1)
                if on[1]:
                    back01(1)
                if on[2]:
                    pe.wait_ge(sem("l2_sum"), this[2])
                    free = bank_free(s, "B", "l2_back_read")
                    if free:
                        pe.wait_ge(*free)
                    for t in range(NT):
                        mm = pe.transpose(bB[:, t * P:(t + 1) * P], yT2[:, t * P:(t + 1) * P], ident)
                    mm.then_inc(sem("l2_back_full"), 1)

            sweep(step_of, pe)

        @block.scalar
        def _(act):
            act.wait_ge(sem("consts"), 16)
            act.wait_ge(sem("setup_v"), 1)

            def step_of(s, par):
                this, past, again = counts(s)
                on = [runs(s, l) for l in range(LAYERS)]

                def leaky(a, hp):
                    act.wait_ge(sem(f"l{a}_offsets"), this[a])
                    if again[a]:
                        act.wait_ge(sem(f"l{a}_sc_p{hp}"), past[a])
                    for t in range(NT):
                        for h in (2 * hp, 2 * hp + 1):
                            last = act.activation(low[a][:, t, h, :], sc[a][:, t, h, :], ACT.Identity,
                                                  bias=off2[a][:, t, h:h + 1], scale=SLOPE)
                    last.then_inc(sem(f"l{a}_leaky_p{hp}"), 1)

                def exps(a, k):
                    m, hp = CHUNKS[k]
                    act.wait_ge(sem(f"l{a}_turned_c{k}"), this[a])
                    if k == 0:
                        if again[a]:
                            act.wait_ge(sem(f"l{a}_agg_full"), past[a])
                    src = (bD, bE)[k % 2]
                    act.activation(pT[a][:, m, 2 * hp:2 * hp + 2, :], src[:].rearrange("p (h n) -> p h n", h=2),
                                   ACT.Exp).then_inc(sem(f"l{a}_exp_c{k}"), 1)

                def sums_out(a):
                    act.wait_ge(sem(f"l{a}_agg_full"), this[a])
                    if again[a]:
                        act.wait_ge(sem(f"l{a}_o_full"), past[a])
                    act.activation(aggT[a][:], bA[:].rearrange("p (k n) -> p k n", k=2), ACT.Copy)\
                        .then_inc(sem(f"l{a}_agg_read"), 1)

                for a in range(2):
                    if on[a]:
                        act.wait_ge(sem(f"l{a}_xT_full"), this[a])
                        if a == 0 and on[1]:
                            act.wait_ge(sem("l1_xT_full"), this[1])
                        if again[a]:
                            act.wait_ge(sem(f"l{a}_he_full"), past[a])
                        act.activation(xT01[:, a, :], bA[:, a * N:(a + 1) * N], ACT.Copy)\
                            .then_inc(sem(f"l{a}_xT_read"), 1)
                if on[2]:
                    act.wait_ge(sem("l2_xT_full"), this[2])
                    if again[2]:
                        act.wait_ge(sem("l2_inhn_full"), past[2])
                    if again[2]:
                        act.wait_ge(sem("l2_blend"), past[2])
                    if again[2]:
                        act.wait_ge(sem("l2_sum"), past[2])
                    act.activation(xT2[:], bC[:, 0:N], ACT.Copy).then_inc(sem("l2_xT_read"), 1)
                    act.wait_ge(sem("l2_adjT_full"), this[2])
                    if again[3]:
                        act.wait_ge(sem("l3_agg_full"), past[3])
                    act.activation(adjT[par][:], bB[:].rearrange("p (t n) -> p t n", t=NT), ACT.Copy)\
                        .then_inc(sem("l2_adjT_read"), 1)
                    act.wait_ge(sem("l2_c1s_full"), this[2])
                    if again[2]:
                        act.wait_ge(sem("l2_conv2_full"), past[2])
                    act.activation(h1[:, PAD:PAD + N], bA[:, 0:N], ACT.Relu, bias=bn_b[:, 0:1],
                                   scale=bn_s[:, 0:1]).then_inc(sem("l2_h1"), 1)
                    if again[2]:
                        act.wait_ge(sem("l2_dist_full"), past[2])
                    act.activation(seL[0:3, :], bA[0:3, N:2 * N], ACT.Identity, bias=bse2[0:3, :], scale=2.0)
                    act.activation(seL[32:35, :], bA[32:35, N:2 * N], ACT.Square, bias=c("bse")[32:35, :])\
                        .then_inc(sem("l2_se"), 1)
                    act.activation(seR[0:3, :], bA[0:3, N:2 * N], ACT.Identity, bias=c("bse")[0:3, :])
                    act.activation(seR[64:67, :], bA[64:67, N:2 * N], ACT.Square, bias=c("bse")[64:67, :])\
                        .then_inc(sem("l2_seR"), 1)
                if on[3]:
                    act.wait_ge(sem("l3_hT_full"), this[3])
                    if again[3]:
                        act.wait_ge(sem("l3_conv_full"), past[3])
                    act.activation(h3T[:], bB[:, 0:N], ACT.Copy).then_inc(sem("l3_hT_read"), 1)
                if on[0]:
                    leaky(0, 0)
                if on[2]:
                    act.wait_ge(sem("l2_dist_full"), this[2])
                    if again[2]:
                        act.wait_ge(sem("l2_aT"), past[2])
                    act.activation(near[:], bA[:].rearrange("p (t n) -> p t n", t=NT), ACT.Exp)\
                        .then_inc(sem("l2_near_ready"), 1)
                if on[0]:
                    leaky(0, 1)
                if on[3]:
                    act.wait_ge(sem("l3_agg_full"), this[3])
                    act.activation(agg3[:], bB[:, 0:N], ACT.Copy).then_inc(sem("l3_agg_read"), 1)
                if on[0]:
                    for k in range(4):
                        exps(0, k)
                if on[0]:
                    sums_out(0)
                if on[1]:
                    leaky(1, 0)
                if on[2]:
                    act.wait_ge(sem("l2_xnmp_full"), this[2])
                    act.activation(xnmp[:], bC[:, 0:N], ACT.Copy).then_inc(sem("l2_xnmp_read"), 1)
                    act.wait_ge(sem("l2_conv2_read"), this[2])
                    act.activation(xconv[:], conv[:], ACT.Relu, bias=bn_b[:, 1:2]).then_inc(sem("l2_xconv"), 1)
                if on[1]:
                    leaky(1, 1)
                    exps(1, 0)
                    exps(1, 1)
                if on[2]:
                    act.wait_ge(sem("l2_rz_full"), this[2])
                    act.activation(tr[:], bC[:, 0:N], ACT.Tanh, bias=brzh[:, 0:1], scale=0.5)\
                        .then_inc(sem("l2_tr"), 1)
                    act.activation(tz[:], bC[:, N:2 * N], ACT.Tanh, bias=brzh[:, 1:2], scale=0.5)\
                        .then_inc(sem("l2_rz_read"), 1)
                if on[1]:
                    exps(1, 2)
                    exps(1, 3)
                if on[2]:
                    act.wait_ge(sem("l2_inhn_read"), this[2])
                    act.activation(nn[:], pn[:], ACT.Tanh, bias=c("bih", 2, 3)).then_inc(sem("l2_nn"), 1)
                if on[1]:
                    sums_out(1)

            sweep(step_of, act)

        @block.gpsimd
        def _(gp):
            nc.gpsimd.memset(eps[:], EPS)
            nc.gpsimd.memset(mhalf[:], -0.5).then_inc(sem("mhalf"), 1)
            gp.wait_ge(sem("mhalf"), 1)
            gp.wait_ge(sem("bn_v"), 1)
            gp.tensor_tensor(bn_r[:], bn_v[:], mhalf[:], ALU.pow).then_inc(sem("bn_r"), 1)

            def rsqrt(k, layer, what, this):
                gp.wait_ge(sem(f"l{layer}_{what}stats"), this[layer])
                gp.tensor_tensor(ve[k][:], mv[k][:, :, 1], eps[:], ALU.add)\
                    .then_inc(sem(f"l{layer}_{what}ve"), 1)
                gp.wait_ge(sem(f"l{layer}_{what}ve"), this[layer])
                gp.tensor_tensor(rstd[k][:], ve[k][:], mhalf[:], ALU.pow).then_inc(sem(f"l{layer}_{what}rstd"), 1)

            def step_of(s, par):
                this, past, again = counts(s)
                if runs(s, 3):
                    rsqrt(4, 3, "in_", this)
                    gp.wait_ge(sem("l3_hn"), this[3])
                    gp.tensor_tensor(hg[:], hn[:], c("gamma").unsqueeze(1).broadcast_to([P, NT, D]), ALU.mult)\
                        .then_inc(sem("l3_hg"), 1)
                    gp.wait_ge(sem("l3_hg"), this[3])
                    if again[3]:
                        gp.wait_ge(sem("l3_agg_full"), past[3])
                    gp.tensor_tensor(h3[:], hg[:], c("beta").unsqueeze(1).broadcast_to([P, NT, D]), ALU.add)\
                        .then_inc(sem("l3_h"), 1)
                if runs(s, 1):
                    if again[0]:
                        gp.wait_ge(sem("l0_x"), past[0])
                    if again[1]:
                        gp.wait_ge(sem("l1_y1a"), past[1])
                    gp.tensor_tensor(xb1[:], x_in[1][par][:], c("bias1").unsqueeze(1).broadcast_to([P, NT, D]),
                                     ALU.add).then_inc(sem("l1_xb"), 1)
                if runs(s, 3):
                    if again[2]:
                        gp.wait_ge(sem("l2_x"), past[2])
                    if again[3]:
                        gp.wait_ge(sem("l3_y"), past[3])
                    gp.tensor_tensor(x2x[:], x_in[3][par][:], x_in[3][par][:], ALU.add).then_inc(sem("l3_x2x"), 1)
                    rsqrt(3, 3, "", this)
                if runs(s, 0):
                    rsqrt(0, 0, "", this)
                if runs(s, 2):
                    gp.wait_ge(sem("l2_o2"), this[2])
                    if again[2]:
                        gp.wait_ge(sem("l2_back_full"), past[2])
                    gp.tensor_tensor(yT2[:], o2[:], xT2[:], ALU.add).then_inc(sem("l2_sum"), 1)
                if runs(s, 1):
                    rsqrt(1, 1, "", this)
                if runs(s, 2):
                    rsqrt(2, 2, "", this)

            sweep(step_of, gp)

        @block.vector
        def _(dve):
            dve.wait_ge(sem("consts"), 16)
            links = [0]

            def link(ins):
                links[0] += 1
                ins.then_inc(sem("setup_chain"), 1)
                dve.wait_ge(sem("setup_chain"), links[0])

            dve.memset(ones[:], 1.0)
            dve.memset(h1[:], 0.0)
            dve.memset(seL[:], 0.0)
            link(dve.memset(seR[:], 0.0))
            dve.memset(seL[64:67, :], -1.0)
            dve.memset(seR[32:35, :], -1.0)
            for k, base in enumerate(("bn1", "bn2")):
                last = dve.tensor_scalar(bn_v[:, k:k + 1], c(base, 3, 4), EPS, None, ALU.add)
            last.then_inc(sem("bn_v"), 1)
            for a in range(2):
                dve.tensor_copy(w_ext[a][:, 0:P], c(f"w{a}"))
                for r, side in enumerate("lr"):
                    last = dve.tensor_tensor(prod[:, 2 * a + r, :], c(f"w{a}"), c(f"a{a}{side}"), ALU.mult)
            link(last)
            for a in range(2):
                dve.tensor_reduce(w_ext[a][:, P:P + 2 * HEADS],
                                  prod[:, 2 * a:2 * a + 2, :].rearrange("p r (h d) -> p (r h) d", d=DH), AX.X, ALU.add)
            dve.tensor_scalar(bse2[:], c("bse"), 2.0, None, ALU.mult)
            dve.tensor_scalar(bhnh[:], c("bhh", 2, 3), 0.5, None, ALU.mult)
            link(dve.tensor_tensor(brz[:], c("bih", 0, 2), c("bhh", 0, 2), ALU.add))
            dve.tensor_scalar(brzh[:], brz[:], 0.5, None, ALU.mult)
            dve.wait_ge(sem("bn_r"), 1)
            for k, base in enumerate(("bn1", "bn2")):
                last = dve.tensor_tensor(bn_s[:, k:k + 1], c(base, 0, 1), bn_r[:, k:k + 1], ALU.mult)
            link(last)
            for k, base in enumerate(("bn1", "bn2")):
                last = dve.tensor_tensor(bn_ms[:, k:k + 1], c(base, 2, 3), bn_s[:, k:k + 1], ALU.mult)
            link(last)
            for k, base in enumerate(("bn1", "bn2")):
                last = dve.tensor_tensor(bn_b[:, k:k + 1], c(base, 1, 2), bn_ms[:, k:k + 1], ALU.subtract)
            last.then_inc(sem("setup_v"), 1)

            def step_of(s, par):
                this, past, again = counts(s)
                on = [runs(s, l) for l in range(LAYERS)]

                def stats(k, layer, what, src):
                    for t in range(NT):
                        last = dve.bn_stats(st[k][:, t, :], src(t))
                    last.then_inc(sem(f"l{layer}_{what}bn"), 1)
                    dve.wait_ge(sem("consts"), 16)
                    dve.wait_ge(sem(f"l{layer}_{what}bn"), this[layer])
                    for t in range(NT):
                        last = dve.bn_aggr(mv[k][:, t, :], st[k][:, t, :])
                    last.then_inc(sem(f"l{layer}_{what}stats"), 1)

                def normalise(k, layer, what, src, dst, done):
                    dve.wait_ge(sem(f"l{layer}_{what}rstd"), this[layer])
                    for t in range(NT):
                        last = dve.tensor_scalar(dst[:, t, :], src(t), mv[k][:, t, 0:1], rstd[k][:, t:t + 1],
                                                 ALU.subtract, ALU.mult)
                    last.then_inc(sem(done), 1)

                def he_copy(a):
                    dve.wait_ge(sem(f"l{a}_he_full"), this[a])
                    if again[a]:
                        dve.wait_ge(sem(f"l{a}_agg_full"), past[a])
                    W = P + 2 * HEADS
                    dve.tensor_copy(he[a][:], (bD, bE)[a][:, 0:NT * W].rearrange("p (t w) -> p t w", t=NT))\
                        .then_inc(sem(f"l{a}_he_read"), 1)

                def maxima(a, hp):
                    edge = edge0 if a == 0 else edge1[1 - par]
                    dve.wait_ge(sem("consts"), 16)
                    dve.wait_ge(sem(f"l{a}_spread_p{hp}"), this[a])
                    if a == 0:
                        dve.wait_ge(sem("l0_edge0"), this[0])
                    if hp == 0:
                        if again[a]:
                            dve.wait_ge(sem(f"l{a}_turned_c3"), past[a])
                    src = (bF, bG)[hp]
                    for t in range(NT):
                        for h in range(2):
                            last = dve.tensor_tensor_reduce(
                                out=sc[a][:, t, 2 * hp + h, :], in0=edge[:, t, :], in1=src[:, h * N:(h + 1) * N],
                                scale=1.0, scalar=-3.0e38, op0=ALU.add, op1=ALU.max,
                                accum_out=rmax[a][:, t, 2 * hp + h:2 * hp + h + 1])
                    last.then_inc(sem(f"l{a}_max_p{hp}"), 1)

                def offsets(a):
                    left = he[a][:, :, P:P + HEADS]
                    dve.wait_ge(sem(f"l{a}_max_p1"), this[a])
                    dve.tensor_tensor(pre[a][:], rmax[a][:], left, ALU.add).then_inc(sem(f"l{a}_pre"), 1)
                    dve.wait_ge(sem(f"l{a}_pre"), this[a])
                    dve.scalar_tensor_tensor(mrow[a][:], pre[a][:], SLOPE, pre[a][:], ALU.mult, ALU.max)\
                        .then_inc(sem(f"l{a}_mrow"), 1)
                    dve.wait_ge(sem(f"l{a}_mrow"), this[a])
                    dve.tensor_tensor(off1[a][:], left, mrow[a][:], ALU.subtract)
                    dve.scalar_tensor_tensor(off2[a][:], left, SLOPE, mrow[a][:], ALU.mult, ALU.subtract)\
                        .then_inc(sem(f"l{a}_offsets"), 1)

                def shift(a, hp):
                    dve.wait_ge(sem(f"l{a}_leaky_p{hp}"), this[a])
                    dve.wait_ge(sem(f"l{a}_offsets"), this[a])
                    for t in range(NT):
                        for h in (2 * hp, 2 * hp + 1):
                            last = dve.scalar_tensor_tensor(sc[a][:, t, h, :], sc[a][:, t, h, :], off1[a][:, t, h:h + 1],
                                                            low[a][:, t, h, :], ALU.add, ALU.max)
                    last.then_inc(sem(f"l{a}_sc_p{hp}"), 1)

                def divide(a):
                    dve.wait_ge(sem(f"l{a}_o_full"), this[a])
                    sums = bA[:, N:2 * N].rearrange("p (t h d) -> p t h d", t=NT, d=DH)
                    dve.reciprocal(rden[a][:], sums[:, :, :, 0]).then_inc(sem(f"l{a}_rden"), 1)
                    dve.wait_ge(sem(f"l{a}_rden"), this[a])
                    dve.tensor_tensor(att[a][:].rearrange("p t (h d) -> p t h d", d=DH),
                                      bA[:, 0:N].rearrange("p (t h d) -> p t h d", t=NT, d=DH),
                                      rden[a][:].unsqueeze(3).broadcast_to([P, NT, HEADS, DH]), ALU.mult)\
                        .then_inc(sem(f"l{a}_o_read"), 1)
                    dve.wait_ge(sem(f"l{a}_o_read"), this[a])

                def tiles(t2):
                    return t2[:, 0:NT * D].rearrange("p (t d) -> p t d", t=NT)

                if on[3]:
                    if again[2]:
                        dve.wait_ge(sem("l2_x"), past[2])
                    stats(4, 3, "in_", lambda t: x_in[3][par][:, t, :])
                if on[0]:
                    dve.wait_ge(sem("l0_loaded"), 32 * this[0])
                    dve.tensor_scalar(edge0[:], adj_a[par][:], 0.0, NEG, ALU.is_le, ALU.mult)\
                        .then_inc(sem("l0_edge0"), 1)
                    dve.tensor_scalar(padmask[:], adj_a[par][:], EPS, NEG, ALU.is_le, ALU.mult)\
                        .then_inc(sem("l0_pad"), 1)
                    dve.wait_ge(sem("l0_pad"), this[0])
                    dve.scalar_tensor_tensor(edge1[par][:], adj_a[par][:], c("we"), padmask[:], ALU.mult, ALU.add)\
                        .then_inc(sem("l0_edge1"), 1)
                    he_copy(0)
                if on[1]:
                    he_copy(1)
                if on[0]:
                    maxima(0, 0)
                    maxima(0, 1)
                    offsets(0)
                if on[3]:
                    if again[3]:
                        dve.wait_ge(sem("l3_h"), past[3])
                    normalise(4, 3, "in_", lambda t: x_in[3][par][:, t, :], hn, "l3_hn")
                if on[0]:
                    shift(0, 0)
                if on[2]:
                    dve.wait_ge(sem("l2_msg_full"), this[2])
                    dve.tensor_tensor(msg_b[:], tiles(bC), c("bmsg").unsqueeze(1).broadcast_to([P, NT, D]), ALU.add)\
                        .then_inc(sem("l2_msg_read"), 1)
                    dve.wait_ge(sem("l2_msg_read"), this[2])
                    if again[2]:
                        dve.wait_ge(sem("l2_xnmp_full"), past[2])
                    dve.tensor_scalar(msg[:], msg_b[:], 0.0, None, ALU.max)
                    dve.wait_ge(sem("l2_near_ready"), this[2])
                    dve.tensor_tensor(aT[:], near[:], adjT[par][:], ALU.mult).then_inc(sem("l2_aT"), 1)
                if on[0]:
                    shift(0, 1)
                if on[1]:
                    maxima(1, 0)
                    maxima(1, 1)
                    offsets(1)
                if on[2]:
                    dve.wait_ge(sem("l2_conv2_full"), this[2])
                    dve.scalar_tensor_tensor(conv[:], bH[:, 0:N], bn_s[:, 1:2], xT2[:], ALU.mult, ALU.add)\
                        .then_inc(sem("l2_conv2_read"), 1)
                if on[3]:
                    dve.wait_ge(sem("l3_conv_full"), this[3])
                    dve.tensor_tensor(cb[:], tiles(bB), c("brel").unsqueeze(1).broadcast_to([P, NT, D]), ALU.add)\
                        .then_inc(sem("l3_conv_read"), 1)
                    dve.wait_ge(sem("l3_conv_read"), this[3])
                    dve.wait_ge(sem("l3_x2x"), this[3])
                    dve.scalar_tensor_tensor(y[3][:], cb[:], 0.0, x2x[:], ALU.max, ALU.add)\
                        .then_inc(sem("l3_y"), 1)
                    dve.wait_ge(sem("l3_y"), this[3])
                    stats(3, 3, "", lambda t: y[3][:, t, :])
                if on[1]:
                    shift(1, 0)
                if on[0]:
                    divide(0)
                    dve.tensor_tensor(y[0][:], att[0][:], x_in[0][par][:], ALU.add).then_inc(sem("l0_sum"), 1)
                if on[1]:
                    shift(1, 1)
                if on[0]:
                    dve.wait_ge(sem("l0_sum"), this[0])
                    stats(0, 0, "", lambda t: y[0][:, t, :])
                if on[3]:
                    if again[3]:
                        dve.wait_ge(sem("l3_stored"), 16 * past[3])
                    normalise(3, 3, "", lambda t: y[3][:, t, :], y_out[par], "l3_out")
                if on[2]:
                    dve.wait_ge(sem("l2_inhn_full"), this[2])
                    dve.tensor_scalar(hb[:], bH[:, N:2 * N], 0.5, bhnh[:, 0:1], ALU.mult, ALU.add)\
                        .then_inc(sem("l2_hb"), 1)
                    dve.wait_ge(sem("l2_hb"), this[2])
                    dve.wait_ge(sem("l2_tr"), this[2])
                    dve.scalar_tensor_tensor(q[:], tr[:], 1.0, hb[:], ALU.add, ALU.mult).then_inc(sem("l2_q"), 1)
                    dve.wait_ge(sem("l2_q"), this[2])
                    dve.tensor_tensor(pn[:], bH[:, 0:N], q[:], ALU.add).then_inc(sem("l2_inhn_read"), 1)
                if on[0]:
                    if again[1]:
                        dve.wait_ge(sem("l1_xT_full"), past[1])
                    normalise(0, 0, "", lambda t: y[0][:, t, :], x_in[1][1 - par], "l0_x")
                if on[2]:
                    dve.wait_ge(sem("l2_nn"), this[2])
                    dve.wait_ge(sem("l2_rz_read"), this[2])
                    dve.tensor_tensor(dl[:], xT2[:], nn[:], ALU.subtract).then_inc(sem("l2_dl"), 1)
                    dve.wait_ge(sem("l2_dl"), this[2])
                    dve.scalar_tensor_tensor(tzd[:], tz[:], 1.0, dl[:], ALU.add, ALU.mult).then_inc(sem("l2_blend"), 1)
                    dve.wait_ge(sem("l2_blend"), this[2])
                    if again[2]:
                        dve.wait_ge(sem("l2_sum"), past[2])
                    dve.scalar_tensor_tensor(o2[:], tzd[:], 0.5, nn[:], ALU.mult, ALU.add).then_inc(sem("l2_o2"), 1)
                if on[1]:
                    divide(1)
                    dve.wait_ge(sem("l1_xb"), this[1])
                    dve.tensor_tensor(y1a[:], att[1][:], xb1[:], ALU.add).then_inc(sem("l1_biased"), 1)
                    dve.wait_ge(sem("l1_biased"), this[1])
                    dve.scalar_tensor_tensor(y1b[:], y1a[:], 0.5, y1a[:], ALU.mult, ALU.max).then_inc(sem("l1_y1a"), 1)
                    dve.wait_ge(sem("l1_y1a"), this[1])
                    dve.tensor_tensor(y[1][:], y1b[:], x_in[1][par][:], ALU.add).then_inc(sem("l1_sum"), 1)
                    dve.wait_ge(sem("l1_sum"), this[1])
                    stats(1, 1, "", lambda t: y[1][:, t, :])
                if on[2]:
                    dve.wait_ge(sem("l2_back_full"), this[2])
                    dve.tensor_copy(y[2][:], tiles(bB)).then_inc(sem("l2_back_read"), 1)
                    dve.wait_ge(sem("l2_back_read"), this[2])
                    stats(2, 2, "", lambda t: y[2][:, t, :])
                if on[1]:
                    if again[2]:
                        dve.wait_ge(sem("l2_xT_full"), past[2])
                    normalise(1, 1, "", lambda t: y[1][:, t, :], x_in[2][1 - par], "l1_x")
                if on[2]:
                    normalise(2, 2, "", lambda t: y[2][:, t, :], x_in[3][1 - par], "l2_x")

            sweep(step_of, dve)


def pack(v):
    def rows(a):
        return np.broadcast_to(np.reshape(a, (1, P)), (P, P))

    def cols(a):
        return np.reshape(a, (-1, P)).T

    wse, bse = np.zeros((P, 96), np.float32), np.zeros((P, 1), np.float32)
    for at in (0, 32, 64):
        wse[:, at:at + 3] = v["L2_gnn_w_se"].T
        bse[at:at + 3, 0] = v["L2_gnn_b_se"]
    a0, a1 = v["L0_gnn_a"], v["L1_gnn_a_w"][0]
    wih = v["L2_gnn_w_ih"]
    parts = {
        "ident": np.eye(P, dtype=np.float32),
        "w0": v["L0_gnn_W"], "w1": v["L1_gnn_W_proj"].T,
        "a0l": rows(a0[:, :DH]), "a0r": rows(a0[:, DH:]),
        "a1l": rows(np.tile(a1[:DH], HEADS)), "a1r": rows(np.tile(a1[DH:2 * DH], HEADS)),
        "bias1": rows(v["L1_gnn_bias"]),
        "conv1": v["L2_gnn_conv1_w"][:, :, 0].T,
        "conv2": v["L2_gnn_conv2_w"].transpose(1, 2, 0).reshape(P, TAPS * P),
        "wmsg": v["L2_gnn_w_msg"].T, "bmsg": rows(v["L2_gnn_b_msg"]), "wse": wse,
        "wih": np.concatenate([wih[:, :P].T, wih[:, P:].T], axis=1), "whh": v["L2_gnn_w_hh"].T,
        "wrel": v["L3_gnn_W_rel"], "wroot": v["L3_gnn_W_root"], "brel": rows(v["L3_gnn_b_rel"]),
        "gamma": rows(v["L3_gnn_ln_gamma"]), "beta": rows(v["L3_gnn_ln_beta"]),
        "bn1": np.stack([v[f"L2_gnn_bn1_{k}"] for k in "gbmv"], axis=1),
        "bn2": np.stack([v[f"L2_gnn_bn2_{k}"] for k in "gbmv"], axis=1),
        "bih": cols(v["L2_gnn_b_ih"]), "bhh": cols(v["L2_gnn_b_hh"]),
        "bse": bse, "we": np.broadcast_to(np.reshape(a1[2 * DH:], (1, 1)), (P, 1)),
    }
    return np.concatenate([parts[name] for name, _ in COLUMNS], axis=1)


def kernel(**inputs):
    import concourse.bacc as bacc
    from concourse.bass_utils import run_bass_kernel_spmd

    v = {name: np.asarray(a) for name, a in inputs.items()}
    arrays = {"in_x": np.ascontiguousarray(v["x"]), "in_adj": np.ascontiguousarray(v["adj"]),
              "in_consts": np.ascontiguousarray(pack(v))}
    nc = bacc.Bacc("TRN2", target_bir_lowering=False, num_devices=1)
    aps = [nc.dram_tensor(name, a.shape, F32, kind="ExternalInput").ap() for name, a in arrays.items()]
    out = nc.dram_tensor("out", v["x"].shape, F32, kind="ExternalOutput").ap()
    build(nc, *aps, out)
    r = run_bass_kernel_spmd(nc, [arrays], core_ids=[0])
    return r.results[0]["out"]
```

```python
from contextlib import ExitStack

import numpy as np

import concourse.bass as bass
from concourse import mybir
from concourse.alu_op_type import AluOpType as ALU

F32 = mybir.dt.float32
ACT = mybir.ActivationFunctionType
AX = mybir.AxisListType

P = 128
HEADS = 4
DH = P // HEADS
NEG = -float(2 ** 53)
SLOPE = 0.2
EPS = 1e-5
TAPS = 17
PAD = TAPS // 2
STAGES = 5
TAIL, TSTAGE = ("l0", "l1t"), (0, 2)
STAGE = {"l0": 0, "l1": 1, "l1t": 2, "l2": 2, "l2t": 3, "l3": 4}

COLUMNS = [
    ("ident", P), ("w0", P), ("w1", P), ("a0l", P), ("a0r", P), ("a1l", P), ("a1r", P), ("bias1", P),
    ("conv1", P), ("conv2", TAPS * P), ("wmsg", P), ("bmsg", P), ("wse", 96),
    ("wih", 6 * P), ("whh", 3 * P), ("wrel", P), ("wroot", P), ("brel", P), ("gamma", P), ("beta", P),
    ("bn1", 4), ("bn2", 4), ("bih", 3), ("bhh", 3), ("bse", 1), ("we", 1),
]
OFFSET, WIDTH = {}, 0
for _name, _n in COLUMNS:
    OFFSET[_name] = (WIDTH, _n)
    WIDTH += _n


def build(nc, x, adj, consts, out):
    B, N, D = x.shape
    NT = N // P
    HN = HEADS * N
    STEPS = B + STAGES - 1

    x_d = x.rearrange("b (t p) d -> b p t d", p=P)
    adj_d = adj.rearrange("b (t p) m -> b p t m", p=P)
    out_d = out.rearrange("b (t p) d -> b p t d", p=P)

    with ExitStack() as ctx:
        def sb(name, shape):
            return ctx.enter_context(nc.sbuf_tensor(name, shape, F32))

        def bank(name):
            return ctx.enter_context(nc.psum_tensor("bank_" + name, [P, 512], F32))

        cst = sb("cst", [P, WIDTH])

        def c(name, a=0, b=None):
            at, n = OFFSET[name]
            return cst[:, at + a:at + (n if b is None else b)]

        ident = c("ident")
        x0 = [sb(f"x0_{p}", [P, NT, D]) for p in range(2)]
        x1 = [sb(f"x1_{p}", [P, NT, D]) for p in range(2)]
        x2 = sb("x2", [P, NT, D])
        x3 = [sb(f"x3_{p}", [P, NT, D]) for p in range(2)]
        adj_a = [sb(f"adj_a{p}", [P, NT, N]) for p in range(2)]
        adj_b = [sb(f"adj_b{p}", [P, NT, N]) for p in range(2)]
        adjT = [sb(f"adjT{p}", [P, NT, N]) for p in range(2)]
        y_out = [sb(f"y_out{p}", [P, NT, D]) for p in range(2)]
        edge0 = sb("edge0", [P, NT, N])
        edge1 = [sb(f"edge1_{p}", [P, NT, N]) for p in range(2)]
        padmask = sb("padmask", [P, NT, N])

        w_ext = [sb(f"w_ext{a}", [P, P + 2 * HEADS]) for a in range(2)]
        prod = sb("prod", [P, 4, P])
        xT01 = sb("xT01", [P, 2, N])
        he = [sb(f"he{a}", [P, NT, P + 2 * HEADS]) for a in range(2)]
        sc = [sb(f"sc{a}", [P, NT, HEADS, N]) for a in range(2)]
        low = [sb(f"low{a}", [P, NT, HEADS, N]) for a in range(2)]
        rmax = [sb(f"rmax{a}", [P, NT, HEADS]) for a in range(2)]
        pre = [sb(f"pre{a}", [P, NT, HEADS]) for a in range(2)]
        mrow = [sb(f"mrow{a}", [P, NT, HEADS]) for a in range(2)]
        off1 = [sb(f"off1_{a}", [P, NT, HEADS]) for a in range(2)]
        off2 = [sb(f"off2_{a}", [P, NT, HEADS]) for a in range(2)]
        pT = [sb(f"pT{a}", [P, NT, HEADS, N]) for a in range(2)]
        ones = sb("ones", [P, DH])
        aggT = [sb(f"aggT{a}", [P, 2, N]) for a in range(2)]
        rden = [sb(f"rden{a}", [P, NT, HEADS]) for a in range(2)]
        att = [sb(f"att{a}", [P, NT, D]) for a in range(2)]
        xb1 = sb("xb1", [P, NT, D])
        y1a = sb("y1a", [P, NT, D])
        y1b = sb("y1b", [P, NT, D])
        y = [sb(f"y{s}", [P, NT, D]) for s in range(5)]
        st = [sb(f"st{s}", [P, NT, 6]) for s in range(5)]
        mv = [sb(f"mv{s}", [P, NT, 2]) for s in range(5)]
        ve = [sb(f"ve{s}", [P, NT]) for s in range(5)]
        rstd = [sb(f"rstd{s}", [P, NT]) for s in range(5)]
        mhalf = sb("mhalf", [P, NT])
        eps = sb("eps", [P, NT])

        xT2 = [sb(f"xT2_{p}", [P, N]) for p in range(2)]
        h1 = sb("h1", [P, N + 2 * PAD])
        seL = sb("seL", [96, N])
        seR = sb("seR", [96, N])
        bse2 = sb("bse2", [P, 1])
        msg_b = sb("msg_b", [P, NT, D])
        msg = sb("msg", [P, NT, D])
        near = sb("near", [P, NT, N])
        aT = sb("aT", [P, NT, N])
        conv = sb("conv", [P, N])
        xconv = sb("xconv", [P, N])
        xnmp = sb("xnmp", [P, N])
        tr = sb("tr", [P, N])
        tz = sb("tz", [P, N])
        hb = sb("hb", [P, N])
        q = sb("q", [P, N])
        pn = sb("pn", [P, N])
        nn = sb("nn", [P, N])
        dl = sb("dl", [P, N])
        tzd = sb("tzd", [P, N])
        o2 = sb("o2", [P, N])
        yT2 = sb("yT2", [P, N])
        bn_v = sb("bn_v", [P, 2])
        bn_r = sb("bn_r", [P, 2])
        bn_s = sb("bn_s", [P, 2])
        bn_ms = sb("bn_ms", [P, 2])
        bn_b = sb("bn_b", [P, 2])
        brz = sb("brz", [P, 2])
        brzh = sb("brzh", [P, 2])
        bhnh = sb("bhnh", [P, 1])

        hn = sb("hn", [P, NT, D])
        hg = sb("hg", [P, NT, D])
        h3 = sb("h3", [P, NT, D])
        h3T = sb("h3T", [P, N])
        agg3 = sb("agg3", [P, N])
        cb = sb("cb", [P, NT, D])
        x2x = sb("x2x", [P, NT, D])

        bA, bB, bC, bD, bE, bF, bG, bH = (bank(n) for n in "ABCDEFGH")

        sems = {}

        def sem(name):
            if name not in sems:
                sems[name] = ctx.enter_context(nc.semaphore(name))
            return sems[name]

        def stage_of(name):
            return STAGE[name.split("_")[0]]

        def runs(step, stage):
            return not isinstance(step, int) or 0 <= step - stage < B

        def counts(step):
            return ([step + 1 - g for g in range(STAGES)], [step - g for g in range(STAGES)],
                    [runs(step - 1, g) for g in range(STAGES)])

        EMPTIED = {
            "A": ["l0_xT_read", "l1t_agg_read", "l1t_o_read", "l0_agg_read", "l0_o_read", "l1_xT_read",
                  "l2_h1", "l2_near"],
            "B": ["l3_hT_read", "l3_agg_read", "l3_conv_read", "l2_adjT_read", "l2t_back_read"],
            "C": ["l2t_xnmp_read", "l2t_rz_read", "l2_xT_read", "l2_msg_read"],
            "D": ["l1t_exp_c0", "l1t_exp_c2", "l0_exp_c0", "l0_exp_c2"],
            "E": ["l1t_exp_c1", "l1t_exp_c3", "l0_exp_c1", "l0_exp_c3"],
            "F": ["l0_he_read", "l0_max_p0", "l1_he_read", "l1_max_p0"],
            "G": ["l0_max_p1", "l1_max_p1"],
            "H": ["l2t_conv2_read", "l2t_inhn_read"],
        }
        CHUNKS = [(0, 0), (1, 0), (0, 1), (1, 1)]

        def bank_free(step, name, mine):
            this, past, again = counts(step)
            uses = EMPTIED[name]
            for other in reversed(uses[:uses.index(mine)]):
                if runs(step, stage_of(other)):
                    return sem(other), this[stage_of(other)]
            for other in reversed(uses):
                if again[stage_of(other)]:
                    return sem(other), past[stage_of(other)]
            return None

        def sweep(eng_steps, eng):
            first = STAGES
            pairs = (B - 1 - first) // 2
            for s in range(first):
                eng_steps(s, s % 2)
            with eng.Fori(0, pairs) as pair:
                eng_steps(pair * 2 + first, first % 2)
                eng_steps(pair * 2 + (first + 1), (first + 1) % 2)
            for s in range(first + 2 * pairs, STEPS):
                eng_steps(s, s % 2)

        block = ctx.enter_context(nc.Block())

        @block.sync
        def _(sp):
            sp.dma_start(x0[0][:], x_d[0]).then_inc(sem("l0_loaded"), 16)
            sp.dma_start(cst[:], consts).then_inc(sem("consts"), 16)
            sp.dma_start(adj_a[0][:], adj_d[0]).then_inc(sem("l0_loaded"), 16)

            def step_of(s, par):
                this, past, again = counts(s)
                if not isinstance(s, int) or s + 1 < B:
                    sp.wait_ge(sem("consts"), 16)
                    if again[0]:
                        sp.wait_ge(sem("l0_sum"), past[0])
                        sp.wait_ge(sem("l0_edge1"), past[0])
                    sp.wait_ge(sem("l0_loaded"), 32 * this[0])
                    sp.dma_start(x0[1 - par][:], x_d[s + 1]).then_inc(sem("l0_loaded"), 16)
                    sp.dma_start(adj_a[1 - par][:], adj_d[s + 1]).then_inc(sem("l0_loaded"), 16)
                if not isinstance(s, int) or 0 <= s - 1 < B:
                    sp.wait_ge(sem("consts"), 16)
                    if again[2]:
                        sp.wait_ge(sem("l2_adjT_read"), past[2])
                    if runs(s, 2):
                        sp.wait_ge(sem("l2_loaded"), 16 * this[2])
                    sp.dma_start(adj_b[1 - par][:], adj_d[s - 1]).then_inc(sem("l2_loaded"), 16)
                if runs(s, 4):
                    sp.wait_ge(sem("consts"), 16)
                    sp.wait_ge(sem("l3_out"), this[4])
                    if again[4]:
                        sp.wait_ge(sem("l3_stored"), 16 * past[4])
                    sp.dma_start(out_d[s - 4], y_out[par][:]).then_inc(sem("l3_stored"), 16)

            sweep(step_of, sp)
            sp.wait_ge(sem("l3_stored"), 16 * B)

        @block.tensor
        def _(pe):
            pe.wait_ge(sem("consts"), 16)
            pe.wait_ge(sem("setup_v"), 1)

            def step_of(s, par):
                this, past, again = counts(s)
                on = [runs(s, g) for g in range(STAGES)]

                def claim(name, mine):
                    free = bank_free(s, name, mine)
                    if free:
                        pe.wait_ge(*free)

                def turn(dst, src):
                    for t in range(NT):
                        mm = pe.transpose(dst[:, t * P:(t + 1) * P], src[:, t, :], ident)
                    return mm

                def inputs01(a):
                    if a == 0:
                        pe.wait_ge(sem("l0_loaded"), 32 * this[0])
                    elif again[0]:
                        pe.wait_ge(sem("l0_x"), past[0])
                    claim("A", f"l{a}_xT_read")
                    turn(bA, (x0, x1)[a][par]).then_inc(sem(f"l{a}_xT_full"), 1)

                def project(a):
                    pe.wait_ge(sem(f"l{a}_xT_read"), this[a])
                    claim("F", f"l{a}_he_read")
                    W = P + 2 * HEADS
                    for t in range(NT):
                        mm = pe.matmul(bF[:, t * W:(t + 1) * W], xT01[:, a, t * P:(t + 1) * P], w_ext[a][:],
                                       start=True, stop=True)
                    mm.then_inc(sem(f"l{a}_he_full"), 1)

                def spread(a):
                    pe.wait_ge(sem(f"l{a}_he_read"), this[a])
                    for hp, (dst, name) in enumerate(((bF, "F"), (bG, "G"))):
                        claim(name, f"l{a}_max_p{hp}")
                        for h in range(2):
                            for t in range(NT):
                                at = P + HEADS + 2 * hp + h
                                mm = pe.transpose(dst[:, h * N + t * P:h * N + (t + 1) * P],
                                                  he[a][:, t, at:at + 1].broadcast_to([P, P]), ident)
                        mm.then_inc(sem(f"l{a}_spread_p{hp}"), 1)

                def turn_scores(a, k):
                    m, hp = CHUNKS[k]
                    dst, name = ((bD, "D"), (bE, "E"))[k % 2]
                    if a == 0:
                        pe.wait_ge(sem(f"l0_sc_p{hp}"), this[0])
                    elif again[1]:
                        pe.wait_ge(sem(f"l1_sc_p{hp}"), past[1])
                    claim(name, f"{TAIL[a]}_exp_c{k}")
                    for h in range(2):
                        for t in range(NT):
                            mm = pe.transpose(dst[:, h * N + t * P:h * N + (t + 1) * P],
                                              sc[a][:, t, 2 * hp + h, m * P:(m + 1) * P], ident)
                    mm.then_inc(sem(f"{TAIL[a]}_turned_c{k}"), 1)

                def aggregate(a):
                    pe.wait_ge(sem(f"{TAIL[a]}_exp_c3"), this[TSTAGE[a]])
                    claim("A", f"{TAIL[a]}_agg_read")
                    for part in range(2):
                        for m in range(NT):
                            for h in range(HEADS):
                                lhs = he[a][:, m, h * DH:(h + 1) * DH] if part == 0 else ones[:]
                                mm = pe.matmul(bA[h * DH:(h + 1) * DH, part * N:(part + 1) * N], lhs,
                                               pT[a][:, m, h, :], start=(m == 0), stop=(m == NT - 1),
                                               skip_group_check=True)
                    mm.then_inc(sem(f"{TAIL[a]}_agg_full"), 1)

                def back01(a):
                    pe.wait_ge(sem(f"{TAIL[a]}_agg_read"), this[TSTAGE[a]])
                    claim("A", f"{TAIL[a]}_o_read")
                    for k in range(2):
                        for t in range(NT):
                            mm = pe.transpose(bA[:, k * N + t * P:k * N + (t + 1) * P],
                                              aggT[a][:, k, t * P:(t + 1) * P], ident)
                    mm.then_inc(sem(f"{TAIL[a]}_o_full"), 1)

                def taps(k0, k1):
                    if k0 == 0:
                        if again[2]:
                            pe.wait_ge(sem("l2_h1"), past[2])
                        claim("H", "l2t_conv2_read")
                    for k in range(k0, k1):
                        mm = pe.matmul(bH[:, 0:N], c("conv2", k * P, (k + 1) * P), h1[:, k:k + N],
                                       start=(k == 0), stop=(k == TAPS - 1), skip_group_check=True)
                    if k1 == TAPS:
                        mm.then_inc(sem("l2t_conv2_full"), 1)

                def gate(dst, g):
                    pe.matmul(dst, c("wih", (3 + g) * P, (4 + g) * P), xnmp[:], start=True, stop=False,
                              skip_group_check=True)
                    if g < 2:
                        pe.matmul(dst, c("whh", g * P, (g + 1) * P), xT2[1 - par][:], start=False, stop=False,
                                  skip_group_check=True)
                    return pe.matmul(dst, c("wih", g * P, (g + 1) * P), xconv[:], start=False, stop=True,
                                     skip_group_check=True)

                if on[0]:
                    inputs01(0)
                if on[3]:
                    taps(0, 2)
                if on[2]:
                    turn_scores(1, 0)
                    turn_scores(1, 1)
                if on[0]:
                    project(0)
                if on[2]:
                    turn_scores(1, 2)
                    turn_scores(1, 3)
                if on[3]:
                    if again[2]:
                        pe.wait_ge(sem("l2_aT"), past[2])
                    claim("C", "l2t_xnmp_read")
                    for m in range(NT):
                        mm = pe.matmul(bC[:, 0:N], msg[:, m, :], aT[:, m, :], start=(m == 0), stop=(m == NT - 1))
                    mm.then_inc(sem("l2t_xnmp_full"), 1)
                if on[0]:
                    spread(0)
                if on[2]:
                    aggregate(1)
                if on[3]:
                    taps(2, 4)
                if on[2]:
                    back01(1)
                if on[4]:
                    pe.wait_ge(sem("l3_h"), this[4])
                    claim("B", "l3_hT_read")
                    turn(bB, h3).then_inc(sem("l3_hT_full"), 1)
                if on[3]:
                    taps(4, 6)
                if on[4]:
                    claim("B", "l3_agg_read")
                    for m in range(NT):
                        mm = pe.matmul(bB[:, 0:N], h3[:, m, :], adjT[par][:, m, :],
                                       start=(m == 0), stop=(m == NT - 1))
                    mm.then_inc(sem("l3_agg_full"), 1)
                if on[3]:
                    taps(6, 9)
                if on[4]:
                    pe.wait_ge(sem("l3_agg_read"), this[4])
                    claim("B", "l3_conv_read")
                    for t in range(NT):
                        pe.matmul(bB[:, t * P:(t + 1) * P], agg3[:, t * P:(t + 1) * P], c("wrel"),
                                  start=True, stop=False)
                        mm = pe.matmul(bB[:, t * P:(t + 1) * P], h3T[:, t * P:(t + 1) * P], c("wroot"),
                                       start=False, stop=True)
                    mm.then_inc(sem("l3_conv_full"), 1)
                if on[3]:
                    taps(9, TAPS)
                if on[0]:
                    turn_scores(0, 0)
                    turn_scores(0, 1)
                if on[3]:
                    pe.wait_ge(sem("l2t_xnmp_read"), this[3])
                    pe.wait_ge(sem("l2t_xconv"), this[3])
                    claim("C", "l2t_rz_read")
                    gate(bC[:, 0:N], 0)
                    gate(bC[:, N:2 * N], 1).then_inc(sem("l2t_rz_full"), 1)
                if on[0]:
                    turn_scores(0, 2)
                    turn_scores(0, 3)
                if on[3]:
                    claim("H", "l2t_inhn_read")
                    gate(bH[:, 0:N], 2)
                    pe.matmul(bH[:, N:2 * N], c("whh", 2 * P, 3 * P), xT2[1 - par][:], start=True, stop=True,
                              skip_group_check=True).then_inc(sem("l2t_inhn_full"), 1)
                if on[2]:
                    pe.wait_ge(sem("l2_loaded"), 16 * this[2])
                    claim("B", "l2_adjT_read")
                    for m in range(NT):
                        for t in range(NT):
                            mm = pe.transpose(bB[:, m * N + t * P:m * N + (t + 1) * P],
                                              adj_b[par][:, t, m * P:(m + 1) * P], ident)
                    mm.then_inc(sem("l2_adjT_full"), 1)
                    pe.wait_ge(sem("l1t_x"), this[2])
                    claim("C", "l2_xT_read")
                    turn(bC, x2).then_inc(sem("l2_xT_full"), 1)
                if on[0]:
                    aggregate(0)
                    back01(0)
                if on[1]:
                    inputs01(1)
                    project(1)
                if on[2]:
                    pe.wait_ge(sem("l2_xT_read"), this[2])
                    claim("C", "l2_msg_read")
                    for t in range(NT):
                        mm = pe.matmul(bC[:, t * P:(t + 1) * P], xT2[par][:, t * P:(t + 1) * P], c("wmsg"),
                                       start=True, stop=True)
                    mm.then_inc(sem("l2_msg_full"), 1)
                    claim("A", "l2_h1")
                    pe.matmul(bA[:, 0:N], c("conv1"), xT2[par][:], start=True, stop=True)
                    pe.matmul(bA[0:96, N:2 * N], c("wse"), xT2[par][:], start=True, stop=True)\
                        .then_inc(sem("l2_c1s_full"), 1)
                if on[1]:
                    spread(1)
                if on[3]:
                    pe.wait_ge(sem("l2t_sum"), this[3])
                    claim("B", "l2t_back_read")
                    for t in range(NT):
                        mm = pe.transpose(bB[:, t * P:(t + 1) * P], yT2[:, t * P:(t + 1) * P], ident)
                    mm.then_inc(sem("l2t_back_full"), 1)
                if on[2]:
                    pe.wait_ge(sem("l2_se"), this[2])
                    claim("A", "l2_near")
                    for t in range(NT):
                        mm = pe.matmul(bA[:, t * N:(t + 1) * N], seL[:, t * P:(t + 1) * P], seR[:],
                                       start=True, stop=True)
                    mm.then_inc(sem("l2_dist_full"), 1)

            sweep(step_of, pe)

        @block.scalar
        def _(act):
            act.wait_ge(sem("consts"), 16)
            act.wait_ge(sem("setup_v"), 1)

            def step_of(s, par):
                this, past, again = counts(s)
                on = [runs(s, g) for g in range(STAGES)]

                def leaky(a, hp):
                    act.wait_ge(sem(f"l{a}_offsets"), this[a])
                    if again[a]:
                        act.wait_ge(sem(f"l{a}_sc_p{hp}"), past[a])
                    for t in range(NT):
                        for h in (2 * hp, 2 * hp + 1):
                            last = act.activation(low[a][:, t, h, :], sc[a][:, t, h, :], ACT.Identity,
                                                  bias=off2[a][:, t, h:h + 1], scale=SLOPE)
                    last.then_inc(sem(f"l{a}_leaky_p{hp}"), 1)

                def exps(a, k):
                    m, hp = CHUNKS[k]
                    g = TSTAGE[a]
                    act.wait_ge(sem(f"{TAIL[a]}_turned_c{k}"), this[g])
                    if k == 0:
                        if again[g]:
                            act.wait_ge(sem(f"{TAIL[a]}_agg_full"), past[g])
                    src = (bD, bE)[k % 2]
                    act.activation(pT[a][:, m, 2 * hp:2 * hp + 2, :], src[:].rearrange("p (h n) -> p h n", h=2),
                                   ACT.Exp).then_inc(sem(f"{TAIL[a]}_exp_c{k}"), 1)

                def sums_out(a):
                    g = TSTAGE[a]
                    act.wait_ge(sem(f"{TAIL[a]}_agg_full"), this[g])
                    if again[g]:
                        act.wait_ge(sem(f"{TAIL[a]}_o_full"), past[g])
                    act.activation(aggT[a][:], bA[:].rearrange("p (k n) -> p k n", k=2), ACT.Copy)\
                        .then_inc(sem(f"{TAIL[a]}_agg_read"), 1)

                def inputs01(a):
                    act.wait_ge(sem(f"l{a}_xT_full"), this[a])
                    if again[a]:
                        act.wait_ge(sem(f"l{a}_he_full"), past[a])
                    act.activation(xT01[:, a, :], bA[:, 0:N], ACT.Copy).then_inc(sem(f"l{a}_xT_read"), 1)

                if on[0]:
                    inputs01(0)
                if on[2]:
                    for k in range(4):
                        exps(1, k)
                if on[3]:
                    act.wait_ge(sem("l2t_xnmp_full"), this[3])
                    if again[3]:
                        act.wait_ge(sem("l2t_inhn_full"), past[3])
                    act.activation(xnmp[:], bC[:, 0:N], ACT.Copy).then_inc(sem("l2t_xnmp_read"), 1)
                if on[2]:
                    sums_out(1)
                if on[4]:
                    act.wait_ge(sem("l3_hT_full"), this[4])
                    if again[4]:
                        act.wait_ge(sem("l3_conv_full"), past[4])
                    act.activation(h3T[:], bB[:, 0:N], ACT.Copy).then_inc(sem("l3_hT_read"), 1)
                if on[0]:
                    leaky(0, 0)
                if on[4]:
                    act.wait_ge(sem("l3_agg_full"), this[4])
                    act.activation(agg3[:], bB[:, 0:N], ACT.Copy).then_inc(sem("l3_agg_read"), 1)
                if on[0]:
                    leaky(0, 1)
                if on[3]:
                    act.wait_ge(sem("l2t_conv2_read"), this[3])
                    act.activation(xconv[:], conv[:], ACT.Relu, bias=bn_b[:, 1:2]).then_inc(sem("l2t_xconv"), 1)
                if on[0]:
                    exps(0, 0)
                    exps(0, 1)
                if on[3]:
                    act.wait_ge(sem("l2t_rz_full"), this[3])
                    act.activation(tr[:], bC[:, 0:N], ACT.Tanh, bias=brzh[:, 0:1], scale=0.5)\
                        .then_inc(sem("l2t_tr"), 1)
                    act.activation(tz[:], bC[:, N:2 * N], ACT.Tanh, bias=brzh[:, 1:2], scale=0.5)\
                        .then_inc(sem("l2t_rz_read"), 1)
                if on[0]:
                    exps(0, 2)
                    exps(0, 3)
                if on[2]:
                    act.wait_ge(sem("l2_adjT_full"), this[2])
                    if on[4]:
                        act.wait_ge(sem("l3_agg_full"), this[4])
                    act.activation(adjT[par][:], bB[:].rearrange("p (t n) -> p t n", t=NT), ACT.Copy)\
                        .then_inc(sem("l2_adjT_read"), 1)
                if on[3]:
                    act.wait_ge(sem("l2t_inhn_read"), this[3])
                    act.activation(nn[:], pn[:], ACT.Tanh, bias=c("bih", 2, 3)).then_inc(sem("l2t_nn"), 1)
                if on[2]:
                    act.wait_ge(sem("l2_xT_full"), this[2])
                    if again[3]:
                        act.wait_ge(sem("l2t_inhn_full"), past[3])
                        act.wait_ge(sem("l2t_blend"), past[3])
                        act.wait_ge(sem("l2t_sum"), past[3])
                    act.activation(xT2[par][:], bC[:, 0:N], ACT.Copy).then_inc(sem("l2_xT_read"), 1)
                if on[0]:
                    sums_out(0)
                if on[1]:
                    inputs01(1)
                if on[2]:
                    act.wait_ge(sem("l2_c1s_full"), this[2])
                    if on[3]:
                        act.wait_ge(sem("l2t_conv2_full"), this[3])
                    if again[2]:
                        act.wait_ge(sem("l2_dist_full"), past[2])
                    act.activation(seL[0:3, :], bA[0:3, N:2 * N], ACT.Identity, bias=bse2[0:3, :], scale=2.0)
                    act.activation(seR[0:3, :], bA[0:3, N:2 * N], ACT.Identity, bias=c("bse")[0:3, :])
                    act.activation(seL[32:35, :], bA[32:35, N:2 * N], ACT.Square, bias=c("bse")[32:35, :])
                    act.activation(seR[64:67, :], bA[64:67, N:2 * N], ACT.Square, bias=c("bse")[64:67, :])\
                        .then_inc(sem("l2_se"), 1)
                    act.activation(h1[:, PAD:PAD + N], bA[:, 0:N], ACT.Relu, bias=bn_b[:, 0:1],
                                   scale=bn_s[:, 0:1]).then_inc(sem("l2_h1"), 1)
                if on[1]:
                    leaky(1, 0)
                if on[2]:
                    act.wait_ge(sem("l2_dist_full"), this[2])
                    if again[2]:
                        act.wait_ge(sem("l2_aT"), past[2])
                    act.activation(near[:], bA[:].rearrange("p (t n) -> p t n", t=NT), ACT.Exp)\
                        .then_inc(sem("l2_near"), 1)
                if on[1]:
                    leaky(1, 1)

            sweep(step_of, act)

        @block.gpsimd
        def _(gp):
            nc.gpsimd.memset(eps[:], EPS)
            nc.gpsimd.memset(mhalf[:], -0.5).then_inc(sem("mhalf"), 1)
            gp.wait_ge(sem("mhalf"), 1)
            gp.wait_ge(sem("bn_v"), 1)
            gp.tensor_tensor(bn_r[:], bn_v[:], mhalf[:], ALU.pow).then_inc(sem("bn_r"), 1)

            def rsqrt(k, what, count):
                gp.wait_ge(sem(f"{what}stats"), count)
                gp.tensor_tensor(ve[k][:], mv[k][:, :, 1], eps[:], ALU.add).then_inc(sem(f"{what}ve"), 1)
                gp.wait_ge(sem(f"{what}ve"), count)
                gp.tensor_tensor(rstd[k][:], ve[k][:], mhalf[:], ALU.pow).then_inc(sem(f"{what}rstd"), 1)

            def step_of(s, par):
                this, past, again = counts(s)
                if runs(s, 2):
                    if again[2]:
                        gp.wait_ge(sem("l1t_biased"), past[2])
                    gp.wait_ge(sem("l0_x"), this[2])
                    gp.tensor_tensor(xb1[:], x1[1 - par][:], c("bias1").unsqueeze(1).broadcast_to([P, NT, D]),
                                     ALU.add).then_inc(sem("l1t_xb"), 1)
                if runs(s, 4):
                    rsqrt(4, "l3_in_", this[4])
                    gp.wait_ge(sem("l3_hn"), this[4])
                    gp.tensor_tensor(hg[:], hn[:], c("gamma").unsqueeze(1).broadcast_to([P, NT, D]), ALU.mult)\
                        .then_inc(sem("l3_hg"), 1)
                    gp.wait_ge(sem("l3_hg"), this[4])
                    if again[4]:
                        gp.wait_ge(sem("l3_agg_full"), past[4])
                    gp.tensor_tensor(h3[:], hg[:], c("beta").unsqueeze(1).broadcast_to([P, NT, D]), ALU.add)\
                        .then_inc(sem("l3_h"), 1)
                if runs(s, 2):
                    rsqrt(1, "l1t_", this[2])
                if runs(s, 4):
                    if again[4]:
                        gp.wait_ge(sem("l3_y"), past[4])
                    gp.tensor_tensor(x2x[:], x3[par][:], x3[par][:], ALU.add).then_inc(sem("l3_x2x"), 1)
                    rsqrt(3, "l3_", this[4])
                if runs(s, 0):
                    rsqrt(0, "l0_", this[0])
                if runs(s, 3):
                    gp.wait_ge(sem("l2t_o2"), this[3])
                    if again[3]:
                        gp.wait_ge(sem("l2t_back_full"), past[3])
                    gp.tensor_tensor(yT2[:], o2[:], xT2[1 - par][:], ALU.add).then_inc(sem("l2t_sum"), 1)
                    rsqrt(2, "l2t_", this[3])

            sweep(step_of, gp)

        @block.vector
        def _(dve):
            dve.wait_ge(sem("consts"), 16)
            links = [0]

            def link(ins):
                links[0] += 1
                ins.then_inc(sem("setup_chain"), 1)
                dve.wait_ge(sem("setup_chain"), links[0])

            dve.memset(ones[:], 1.0)
            dve.memset(h1[:], 0.0)
            dve.memset(seL[:], 0.0)
            link(dve.memset(seR[:], 0.0))
            dve.memset(seL[64:67, :], -1.0)
            dve.memset(seR[32:35, :], -1.0)
            for k, base in enumerate(("bn1", "bn2")):
                last = dve.tensor_scalar(bn_v[:, k:k + 1], c(base, 3, 4), EPS, None, ALU.add)
            last.then_inc(sem("bn_v"), 1)
            for a in range(2):
                dve.tensor_copy(w_ext[a][:, 0:P], c(f"w{a}"))
                for r, side in enumerate("lr"):
                    last = dve.tensor_tensor(prod[:, 2 * a + r, :], c(f"w{a}"), c(f"a{a}{side}"), ALU.mult)
            link(last)
            for a in range(2):
                dve.tensor_reduce(w_ext[a][:, P:P + 2 * HEADS],
                                  prod[:, 2 * a:2 * a + 2, :].rearrange("p r (h d) -> p (r h) d", d=DH), AX.X, ALU.add)
            dve.tensor_scalar(bse2[:], c("bse"), 2.0, None, ALU.mult)
            dve.tensor_scalar(bhnh[:], c("bhh", 2, 3), 0.5, None, ALU.mult)
            link(dve.tensor_tensor(brz[:], c("bih", 0, 2), c("bhh", 0, 2), ALU.add))
            dve.tensor_scalar(brzh[:], brz[:], 0.5, None, ALU.mult)
            dve.wait_ge(sem("bn_r"), 1)
            for k, base in enumerate(("bn1", "bn2")):
                last = dve.tensor_tensor(bn_s[:, k:k + 1], c(base, 0, 1), bn_r[:, k:k + 1], ALU.mult)
            link(last)
            for k, base in enumerate(("bn1", "bn2")):
                last = dve.tensor_tensor(bn_ms[:, k:k + 1], c(base, 2, 3), bn_s[:, k:k + 1], ALU.mult)
            link(last)
            for k, base in enumerate(("bn1", "bn2")):
                last = dve.tensor_tensor(bn_b[:, k:k + 1], c(base, 1, 2), bn_ms[:, k:k + 1], ALU.subtract)
            last.then_inc(sem("setup_v"), 1)

            def step_of(s, par):
                this, past, again = counts(s)
                on = [runs(s, g) for g in range(STAGES)]

                def stats(k, what, count, src):
                    for t in range(NT):
                        last = dve.bn_stats(st[k][:, t, :], src(t))
                    last.then_inc(sem(f"{what}bn"), 1)
                    dve.wait_ge(sem("consts"), 16)
                    dve.wait_ge(sem(f"{what}bn"), count)
                    for t in range(NT):
                        last = dve.bn_aggr(mv[k][:, t, :], st[k][:, t, :])
                    last.then_inc(sem(f"{what}stats"), 1)

                def normalise(k, what, count, src, dst, done):
                    dve.wait_ge(sem(f"{what}rstd"), count)
                    for t in range(NT):
                        last = dve.tensor_scalar(dst[:, t, :], src(t), mv[k][:, t, 0:1], rstd[k][:, t:t + 1],
                                                 ALU.subtract, ALU.mult)
                    last.then_inc(sem(done), 1)

                def he_copy(a):
                    dve.wait_ge(sem(f"l{a}_he_full"), this[a])
                    if a == 0 and again[0]:
                        dve.wait_ge(sem("l0_agg_full"), past[0])
                    if a == 1 and on[2]:
                        dve.wait_ge(sem("l1t_agg_full"), this[2])
                    W = P + 2 * HEADS
                    dve.tensor_copy(he[a][:], bF[:, 0:NT * W].rearrange("p (t w) -> p t w", t=NT))\
                        .then_inc(sem(f"l{a}_he_read"), 1)

                def maxima(a, hp):
                    edge = edge0 if a == 0 else edge1[1 - par]
                    dve.wait_ge(sem("consts"), 16)
                    dve.wait_ge(sem(f"l{a}_spread_p{hp}"), this[a])
                    if a == 0:
                        dve.wait_ge(sem("l0_edge0"), this[0])
                    if a == 0 and again[0]:
                        dve.wait_ge(sem(f"l0_turned_c{2 * hp + 1}"), past[0])
                    if a == 1 and on[2]:
                        dve.wait_ge(sem(f"l1t_turned_c{2 * hp + 1}"), this[2])
                    src = (bF, bG)[hp]
                    for t in range(NT):
                        for h in range(2):
                            last = dve.tensor_tensor_reduce(
                                out=sc[a][:, t, 2 * hp + h, :], in0=edge[:, t, :], in1=src[:, h * N:(h + 1) * N],
                                scale=1.0, scalar=-3.0e38, op0=ALU.add, op1=ALU.max,
                                accum_out=rmax[a][:, t, 2 * hp + h:2 * hp + h + 1])
                    last.then_inc(sem(f"l{a}_max_p{hp}"), 1)

                def offsets(a):
                    left = he[a][:, :, P:P + HEADS]
                    dve.wait_ge(sem(f"l{a}_max_p1"), this[a])
                    dve.tensor_tensor(pre[a][:], rmax[a][:], left, ALU.add).then_inc(sem(f"l{a}_pre"), 1)
                    dve.wait_ge(sem(f"l{a}_pre"), this[a])
                    dve.scalar_tensor_tensor(mrow[a][:], pre[a][:], SLOPE, pre[a][:], ALU.mult, ALU.max)\
                        .then_inc(sem(f"l{a}_mrow"), 1)
                    dve.wait_ge(sem(f"l{a}_mrow"), this[a])
                    dve.tensor_tensor(off1[a][:], left, mrow[a][:], ALU.subtract)
                    dve.scalar_tensor_tensor(off2[a][:], left, SLOPE, mrow[a][:], ALU.mult, ALU.subtract)\
                        .then_inc(sem(f"l{a}_offsets"), 1)

                def shift(a, hp):
                    dve.wait_ge(sem(f"l{a}_leaky_p{hp}"), this[a])
                    dve.wait_ge(sem(f"l{a}_offsets"), this[a])
                    for t in range(NT):
                        for h in (2 * hp, 2 * hp + 1):
                            last = dve.scalar_tensor_tensor(sc[a][:, t, h, :], sc[a][:, t, h, :], off1[a][:, t, h:h + 1],
                                                            low[a][:, t, h, :], ALU.add, ALU.max)
                    last.then_inc(sem(f"l{a}_sc_p{hp}"), 1)

                def divide(a):
                    g = TSTAGE[a]
                    dve.wait_ge(sem(f"{TAIL[a]}_o_full"), this[g])
                    sums = bA[:, N:2 * N].rearrange("p (t h d) -> p t h d", t=NT, d=DH)
                    dve.reciprocal(rden[a][:], sums[:, :, :, 0]).then_inc(sem(f"{TAIL[a]}_rden"), 1)
                    dve.wait_ge(sem(f"{TAIL[a]}_rden"), this[g])
                    dve.tensor_tensor(att[a][:].rearrange("p t (h d) -> p t h d", d=DH),
                                      bA[:, 0:N].rearrange("p (t h d) -> p t h d", t=NT, d=DH),
                                      rden[a][:].unsqueeze(3).broadcast_to([P, NT, HEADS, DH]), ALU.mult)\
                        .then_inc(sem(f"{TAIL[a]}_o_read"), 1)
                    dve.wait_ge(sem(f"{TAIL[a]}_o_read"), this[g])

                def tiles(t2):
                    return t2[:, 0:NT * D].rearrange("p (t d) -> p t d", t=NT)

                if on[4]:
                    if again[3]:
                        dve.wait_ge(sem("l2t_x"), past[3])
                    stats(4, "l3_in_", this[4], lambda t: x3[par][:, t, :])
                if on[0]:
                    dve.wait_ge(sem("l0_loaded"), 32 * this[0])
                    dve.tensor_scalar(edge0[:], adj_a[par][:], 0.0, NEG, ALU.is_le, ALU.mult)\
                        .then_inc(sem("l0_edge0"), 1)
                    dve.tensor_scalar(padmask[:], adj_a[par][:], EPS, NEG, ALU.is_le, ALU.mult)\
                        .then_inc(sem("l0_pad"), 1)
                    dve.wait_ge(sem("l0_pad"), this[0])
                    dve.scalar_tensor_tensor(edge1[par][:], adj_a[par][:], c("we"), padmask[:], ALU.mult, ALU.add)\
                        .then_inc(sem("l0_edge1"), 1)
                    he_copy(0)
                if on[4]:
                    if again[4]:
                        dve.wait_ge(sem("l3_h"), past[4])
                    normalise(4, "l3_in_", this[4], lambda t: x3[par][:, t, :], hn, "l3_hn")
                if on[0]:
                    maxima(0, 0)
                    maxima(0, 1)
                    offsets(0)
                if on[2]:
                    divide(1)
                    dve.wait_ge(sem("l1t_xb"), this[2])
                    dve.tensor_tensor(y1a[:], att[1][:], xb1[:], ALU.add).then_inc(sem("l1t_biased"), 1)
                    dve.wait_ge(sem("l1t_biased"), this[2])
                    dve.scalar_tensor_tensor(y1b[:], y1a[:], 0.5, y1a[:], ALU.mult, ALU.max).then_inc(sem("l1t_leaky"), 1)
                    dve.wait_ge(sem("l1t_leaky"), this[2])
                    dve.tensor_tensor(y[1][:], y1b[:], x1[1 - par][:], ALU.add).then_inc(sem("l1t_sum"), 1)
                    dve.wait_ge(sem("l1t_sum"), this[2])
                    stats(1, "l1t_", this[2], lambda t: y[1][:, t, :])
                if on[0]:
                    shift(0, 0)
                    shift(0, 1)
                if on[2]:
                    if again[2]:
                        dve.wait_ge(sem("l2_xT_full"), past[2])
                    normalise(1, "l1t_", this[2], lambda t: y[1][:, t, :], x2, "l1t_x")
                if on[3]:
                    dve.wait_ge(sem("l2t_conv2_full"), this[3])
                    dve.scalar_tensor_tensor(conv[:], bH[:, 0:N], bn_s[:, 1:2], xT2[1 - par][:], ALU.mult, ALU.add)\
                        .then_inc(sem("l2t_conv2_read"), 1)
                if on[4]:
                    dve.wait_ge(sem("l3_conv_full"), this[4])
                    dve.tensor_tensor(cb[:], tiles(bB), c("brel").unsqueeze(1).broadcast_to([P, NT, D]), ALU.add)\
                        .then_inc(sem("l3_conv_read"), 1)
                    dve.wait_ge(sem("l3_conv_read"), this[4])
                    dve.wait_ge(sem("l3_x2x"), this[4])
                    dve.scalar_tensor_tensor(y[3][:], cb[:], 0.0, x2x[:], ALU.max, ALU.add)\
                        .then_inc(sem("l3_y"), 1)
                    dve.wait_ge(sem("l3_y"), this[4])
                    stats(3, "l3_", this[4], lambda t: y[3][:, t, :])
                if on[3]:
                    dve.wait_ge(sem("l2t_inhn_full"), this[3])
                    dve.tensor_scalar(hb[:], bH[:, N:2 * N], 0.5, bhnh[:, 0:1], ALU.mult, ALU.add)\
                        .then_inc(sem("l2t_hb"), 1)
                    dve.wait_ge(sem("l2t_hb"), this[3])
                    dve.wait_ge(sem("l2t_tr"), this[3])
                    dve.scalar_tensor_tensor(q[:], tr[:], 1.0, hb[:], ALU.add, ALU.mult).then_inc(sem("l2t_q"), 1)
                    dve.wait_ge(sem("l2t_q"), this[3])
                    dve.tensor_tensor(pn[:], bH[:, 0:N], q[:], ALU.add).then_inc(sem("l2t_inhn_read"), 1)
                if on[0]:
                    divide(0)
                    dve.tensor_tensor(y[0][:], att[0][:], x0[par][:], ALU.add).then_inc(sem("l0_sum"), 1)
                    dve.wait_ge(sem("l0_sum"), this[0])
                    stats(0, "l0_", this[0], lambda t: y[0][:, t, :])
                if on[4]:
                    if again[4]:
                        dve.wait_ge(sem("l3_stored"), 16 * past[4])
                    normalise(3, "l3_", this[4], lambda t: y[3][:, t, :], y_out[par], "l3_out")
                if on[3]:
                    dve.wait_ge(sem("l2t_nn"), this[3])
                    dve.wait_ge(sem("l2t_rz_read"), this[3])
                    dve.tensor_tensor(dl[:], xT2[1 - par][:], nn[:], ALU.subtract).then_inc(sem("l2t_dl"), 1)
                    dve.wait_ge(sem("l2t_dl"), this[3])
                    dve.scalar_tensor_tensor(tzd[:], tz[:], 1.0, dl[:], ALU.add, ALU.mult)\
                        .then_inc(sem("l2t_blend"), 1)
                    dve.wait_ge(sem("l2t_blend"), this[3])
                    if again[3]:
                        dve.wait_ge(sem("l2t_sum"), past[3])
                    dve.scalar_tensor_tensor(o2[:], tzd[:], 0.5, nn[:], ALU.mult, ALU.add)\
                        .then_inc(sem("l2t_o2"), 1)
                if on[1]:
                    he_copy(1)
                if on[0]:
                    if again[1]:
                        dve.wait_ge(sem("l1_xT_full"), past[1])
                    normalise(0, "l0_", this[0], lambda t: y[0][:, t, :], x1[1 - par], "l0_x")
                if on[1]:
                    maxima(1, 0)
                    maxima(1, 1)
                    offsets(1)
                if on[2]:
                    dve.wait_ge(sem("l2_msg_full"), this[2])
                    dve.tensor_tensor(msg_b[:], tiles(bC), c("bmsg").unsqueeze(1).broadcast_to([P, NT, D]), ALU.add)\
                        .then_inc(sem("l2_msg_read"), 1)
                    dve.wait_ge(sem("l2_msg_read"), this[2])
                    if on[3]:
                        dve.wait_ge(sem("l2t_xnmp_full"), this[3])
                    dve.tensor_scalar(msg[:], msg_b[:], 0.0, None, ALU.max)
                if on[3]:
                    dve.wait_ge(sem("l2t_back_full"), this[3])
                    dve.tensor_copy(y[2][:], tiles(bB)).then_inc(sem("l2t_back_read"), 1)
                    dve.wait_ge(sem("l2t_back_read"), this[3])
                    stats(2, "l2t_", this[3], lambda t: y[2][:, t, :])
                if on[1]:
                    shift(1, 0)
                if on[2]:
                    dve.wait_ge(sem("l2_near"), this[2])
                    dve.wait_ge(sem("l2_adjT_read"), this[2])
                    if on[3]:
                        dve.wait_ge(sem("l2t_xnmp_full"), this[3])
                    dve.tensor_tensor(aT[:], near[:], adjT[par][:], ALU.mult).then_inc(sem("l2_aT"), 1)
                if on[1]:
                    shift(1, 1)
                if on[3]:
                    normalise(2, "l2t_", this[3], lambda t: y[2][:, t, :], x3[1 - par], "l2t_x")

            sweep(step_of, dve)


def pack(v):
    def rows(a):
        return np.broadcast_to(np.reshape(a, (1, P)), (P, P))

    def cols(a):
        return np.reshape(a, (-1, P)).T

    wse, bse = np.zeros((P, 96), np.float32), np.zeros((P, 1), np.float32)
    for at in (0, 32, 64):
        wse[:, at:at + 3] = v["L2_gnn_w_se"].T
        bse[at:at + 3, 0] = v["L2_gnn_b_se"]
    a0, a1 = v["L0_gnn_a"], v["L1_gnn_a_w"][0]
    wih = v["L2_gnn_w_ih"]
    parts = {
        "ident": np.eye(P, dtype=np.float32),
        "w0": v["L0_gnn_W"], "w1": v["L1_gnn_W_proj"].T,
        "a0l": rows(a0[:, :DH]), "a0r": rows(a0[:, DH:]),
        "a1l": rows(np.tile(a1[:DH], HEADS)), "a1r": rows(np.tile(a1[DH:2 * DH], HEADS)),
        "bias1": rows(v["L1_gnn_bias"]),
        "conv1": v["L2_gnn_conv1_w"][:, :, 0].T,
        "conv2": v["L2_gnn_conv2_w"].transpose(1, 2, 0).reshape(P, TAPS * P),
        "wmsg": v["L2_gnn_w_msg"].T, "bmsg": rows(v["L2_gnn_b_msg"]), "wse": wse,
        "wih": np.concatenate([wih[:, :P].T, wih[:, P:].T], axis=1), "whh": v["L2_gnn_w_hh"].T,
        "wrel": v["L3_gnn_W_rel"], "wroot": v["L3_gnn_W_root"], "brel": rows(v["L3_gnn_b_rel"]),
        "gamma": rows(v["L3_gnn_ln_gamma"]), "beta": rows(v["L3_gnn_ln_beta"]),
        "bn1": np.stack([v[f"L2_gnn_bn1_{k}"] for k in "gbmv"], axis=1),
        "bn2": np.stack([v[f"L2_gnn_bn2_{k}"] for k in "gbmv"], axis=1),
        "bih": cols(v["L2_gnn_b_ih"]), "bhh": cols(v["L2_gnn_b_hh"]),
        "bse": bse, "we": np.broadcast_to(np.reshape(a1[2 * DH:], (1, 1)), (P, 1)),
    }
    return np.concatenate([parts[name] for name, _ in COLUMNS], axis=1)


def kernel(**inputs):
    import concourse.bacc as bacc
    from concourse.bass_utils import run_bass_kernel_spmd

    v = {name: np.asarray(a) for name, a in inputs.items()}
    arrays = {"in_x": np.ascontiguousarray(v["x"]), "in_adj": np.ascontiguousarray(v["adj"]),
              "in_consts": np.ascontiguousarray(pack(v))}
    nc = bacc.Bacc("TRN2", target_bir_lowering=False, num_devices=1)
    aps = [nc.dram_tensor(name, a.shape, F32, kind="ExternalInput").ap() for name, a in arrays.items()]
    out = nc.dram_tensor("out", v["x"].shape, F32, kind="ExternalOutput").ap()
    build(nc, *aps, out)
    r = run_bass_kernel_spmd(nc, [arrays], core_ids=[0])
    return r.results[0]["out"]
```

```python
from contextlib import ExitStack

import numpy as np

import concourse.bass as bass
from concourse import mybir
from concourse.alu_op_type import AluOpType as ALU

F32 = mybir.dt.float32
F32R = mybir.dt.float32r
ACT = mybir.ActivationFunctionType
AX = mybir.AxisListType

P = 128
HEADS = 4
DH = P // HEADS
NEG = -float(2 ** 53)
SLOPE = 0.2
EPS = 1e-5
TAPS = 17
PAD = TAPS // 2
STAGES = 5
TAIL, TSTAGE = ("l0", "l1t"), (0, 2)
STAGE = {"l0": 0, "l1": 1, "l1t": 2, "l2": 2, "l2t": 3, "l3": 4}

COLUMNS = [
    ("ident", P), ("w0", P), ("w1", P), ("a0l", P), ("a0r", P), ("a1l", P), ("a1r", P), ("bias1", P),
    ("conv1", P), ("wmsg", P), ("bmsg", P), ("wse", 96),
    ("wrel", P), ("wroot", P), ("brel", P), ("gamma", P), ("beta", P),
    ("bn1", 4), ("bn2", 4), ("bih", 3), ("bhh", 3), ("bse", 1), ("we", 1),
    ("conv2", TAPS * P), ("wih", 6 * P), ("whh", 3 * P),
]
OFFSET, WIDTH = {}, 0
for _name, _n in COLUMNS:
    OFFSET[_name] = (WIDTH, _n)
    WIDTH += _n
EARLY = OFFSET["bias1"][0]
SPLIT = OFFSET["conv2"][0]


def build(nc, x, adj, consts, out):
    B, N, D = x.shape
    NT = N // P
    HN = HEADS * N
    STEPS = B + STAGES - 1

    x_d = x.rearrange("b (t p) d -> b p t d", p=P)
    adj_d = adj.rearrange("b (t p) m -> b p t m", p=P)
    out_d = out.rearrange("b (t p) d -> b p t d", p=P)

    with ExitStack() as ctx:
        def sb(name, shape, dtype=F32):
            return ctx.enter_context(nc.sbuf_tensor(name, shape, dtype))

        def halves(name, width):
            return sb(name + "_hi", [P, width], F32R), sb(name + "_lo", [P, width], F32R)

        def bank(name):
            return ctx.enter_context(nc.psum_tensor("bank_" + name, [P, 512], F32))

        cst = sb("cst", [P, WIDTH])

        def c(name, a=0, b=None):
            at, n = OFFSET[name]
            return cst[:, at + a:at + (n if b is None else b)]

        ident = c("ident")
        x0 = [sb(f"x0_{p}", [P, NT, D]) for p in range(2)]
        x1 = [sb(f"x1_{p}", [P, NT, D]) for p in range(2)]
        x2 = sb("x2", [P, NT, D])
        x3 = [sb(f"x3_{p}", [P, NT, D]) for p in range(2)]
        adj_a = [sb(f"adj_a{p}", [P, NT, N]) for p in range(2)]
        adj_b = [sb(f"adj_b{p}", [P, NT, N]) for p in range(2)]
        adjT = [sb(f"adjT{p}", [P, NT, N]) for p in range(2)]
        y_out = [sb(f"y_out{p}", [P, NT, D]) for p in range(2)]
        edge0 = sb("edge0", [P, NT, N])
        edge1 = [sb(f"edge1_{p}", [P, NT, N]) for p in range(2)]
        padmask = sb("padmask", [P, NT, N])

        w_ext = [sb(f"w_ext{a}", [P, P + 2 * HEADS]) for a in range(2)]
        prod = sb("prod", [P, 4, P])
        xT01 = sb("xT01", [P, 2, N])
        he = [sb(f"he{a}", [P, NT, P + 2 * HEADS]) for a in range(2)]
        sc = [sb(f"sc{a}", [P, NT, HEADS, N]) for a in range(2)]
        low = [sb(f"low{a}", [P, NT, HEADS, N]) for a in range(2)]
        rmax = [sb(f"rmax{a}", [P, NT, HEADS]) for a in range(2)]
        pre = [sb(f"pre{a}", [P, NT, HEADS]) for a in range(2)]
        mrow = [sb(f"mrow{a}", [P, NT, HEADS]) for a in range(2)]
        off1 = [sb(f"off1_{a}", [P, NT, HEADS]) for a in range(2)]
        off2 = [sb(f"off2_{a}", [P, NT, HEADS]) for a in range(2)]
        pT = [sb(f"pT{a}", [P, NT, HEADS, N]) for a in range(2)]
        ones = sb("ones", [P, DH])
        aggT = [sb(f"aggT{a}", [P, 2, N]) for a in range(2)]
        rden = [sb(f"rden{a}", [P, NT, HEADS]) for a in range(2)]
        att = [sb(f"att{a}", [P, NT, D]) for a in range(2)]
        xb1 = sb("xb1", [P, NT, D])
        y1a = sb("y1a", [P, NT, D])
        y1b = sb("y1b", [P, NT, D])
        y = [sb(f"y{s}", [P, NT, D]) for s in range(5)]
        st = [sb(f"st{s}", [P, NT, 6]) for s in range(5)]
        mv = [sb(f"mv{s}", [P, NT, 2]) for s in range(5)]
        ve = [sb(f"ve{s}", [P, NT]) for s in range(5)]
        rstd = [sb(f"rstd{s}", [P, NT]) for s in range(5)]
        mhalf = sb("mhalf", [P, NT])
        eps = sb("eps", [P, NT])

        xT2 = [sb(f"xT2_{p}", [P, N]) for p in range(2)]
        w_parts = halves("w", WIDTH - SPLIT)
        h1_parts = halves("h1", N + 2 * PAD)
        x_parts = [halves(f"xT2_{p}", N) for p in range(2)]
        xconv_parts = halves("xconv", N)
        xnmp_parts = halves("xnmp", N)
        h1 = sb("h1", [P, N + 2 * PAD])
        seL = sb("seL", [96, N])
        seR = sb("seR", [96, N])
        bse2 = sb("bse2", [P, 1])
        msg_b = sb("msg_b", [P, NT, D])
        msg = sb("msg", [P, NT, D])
        near = sb("near", [P, NT, N])
        aT = sb("aT", [P, NT, N])
        conv = sb("conv", [P, N])
        xconv = sb("xconv", [P, N])
        xnmp = sb("xnmp", [P, N])
        tr = sb("tr", [P, N])
        tz = sb("tz", [P, N])
        hb = sb("hb", [P, N])
        q = sb("q", [P, N])
        pn = sb("pn", [P, N])
        nn = sb("nn", [P, N])
        dl = sb("dl", [P, N])
        tzd = sb("tzd", [P, N])
        o2 = sb("o2", [P, N])
        yT2 = sb("yT2", [P, N])
        bn_v = sb("bn_v", [P, 2])
        bn_r = sb("bn_r", [P, 2])
        bn_s = sb("bn_s", [P, 2])
        bn_ms = sb("bn_ms", [P, 2])
        bn_b = sb("bn_b", [P, 2])
        brz = sb("brz", [P, 2])
        brzh = sb("brzh", [P, 2])
        bhnh = sb("bhnh", [P, 1])

        hn = sb("hn", [P, NT, D])
        hg = sb("hg", [P, NT, D])
        h3 = sb("h3", [P, NT, D])
        h3T = sb("h3T", [P, N])
        agg3 = sb("agg3", [P, N])
        cb = sb("cb", [P, NT, D])
        x2x = sb("x2x", [P, NT, D])

        bA, bB, bC, bD, bE, bF, bG, bH = (bank(n) for n in "ABCDEFGH")

        sems = {}

        def sem(name):
            if name not in sems:
                sems[name] = ctx.enter_context(nc.semaphore(name))
            return sems[name]

        def stage_of(name):
            return STAGE[name.split("_")[0]]

        def runs(step, stage):
            return not isinstance(step, int) or 0 <= step - stage < B

        def counts(step):
            return ([step + 1 - g for g in range(STAGES)], [step - g for g in range(STAGES)],
                    [runs(step - 1, g) for g in range(STAGES)])

        EMPTIED = {
            "A": ["l0_xT_read", "l1t_agg_read", "l1t_o_read", "l0_agg_read", "l0_o_read"],
            "B": ["l3_hT_read", "l3_agg_read", "l2_adjT_read", "l3_conv_read", "l2t_back_read"],
            "C": ["l2t_xnmp_read", "l2t_rz_read", "l2_xT_read", "l2_msg_read"],
            "D": ["l1_xT_read", "l1t_exp_c0", "l1t_exp_c2", "l0_exp_c0", "l0_exp_c2", "l2_near"],
            "E": ["l1t_exp_c1", "l1t_exp_c3", "l0_exp_c1", "l0_exp_c3", "l2_h1"],
            "F": ["l0_he_read", "l0_max_p0", "l1_he_read", "l1_max_p0"],
            "G": ["l0_max_p1", "l1_max_p1"],
            "H": ["l2t_conv2_read", "l2t_inhn_read"],
        }
        CHUNKS = [(0, 0), (1, 0), (0, 1), (1, 1)]

        def bank_free(step, name, mine):
            this, past, again = counts(step)
            uses = EMPTIED[name]
            for other in reversed(uses[:uses.index(mine)]):
                if runs(step, stage_of(other)):
                    return sem(other), this[stage_of(other)]
            for other in reversed(uses):
                if again[stage_of(other)]:
                    return sem(other), past[stage_of(other)]
            return None

        def sweep(eng_steps, eng):
            first = STAGES
            pairs = (B - 1 - first) // 2
            for s in range(first):
                eng_steps(s, s % 2)
            with eng.Fori(0, pairs) as pair:
                eng_steps(pair * 2 + first, first % 2)
                eng_steps(pair * 2 + (first + 1), (first + 1) % 2)
            for s in range(first + 2 * pairs, STEPS):
                eng_steps(s, s % 2)

        block = ctx.enter_context(nc.Block())

        @block.sync
        def _(sp):
            sp.dma_start(x0[0][:], x_d[0]).then_inc(sem("l0_loaded"), 16)
            sp.dma_start(cst[:, 0:EARLY], consts[:, 0:EARLY]).then_inc(sem("early_consts"), 16)
            sp.dma_start(cst[:, EARLY:SPLIT], consts[:, EARLY:SPLIT]).then_inc(sem("consts"), 16)
            sp.dma_start(adj_a[0][:], adj_d[0]).then_inc(sem("l0_loaded"), 16)
            sp.dma_start(cst[:, SPLIT:WIDTH], consts[:, SPLIT:WIDTH]).then_inc(sem("late_consts"), 16)

            def step_of(s, par):
                this, past, again = counts(s)
                if not isinstance(s, int) or s + 1 < B:
                    sp.wait_ge(sem("consts"), 16)
                    if again[0]:
                        sp.wait_ge(sem("l0_sum"), past[0])
                        sp.wait_ge(sem("l0_edge1"), past[0])
                    sp.wait_ge(sem("l0_loaded"), 32 * this[0])
                    sp.dma_start(x0[1 - par][:], x_d[s + 1]).then_inc(sem("l0_loaded"), 16)
                    sp.dma_start(adj_a[1 - par][:], adj_d[s + 1]).then_inc(sem("l0_loaded"), 16)
                if not isinstance(s, int) or 0 <= s - 1 < B:
                    sp.wait_ge(sem("consts"), 16)
                    if again[2]:
                        sp.wait_ge(sem("l2_adjT_read"), past[2])
                    if runs(s, 2):
                        sp.wait_ge(sem("l2_loaded"), 16 * this[2])
                    sp.dma_start(adj_b[1 - par][:], adj_d[s - 1]).then_inc(sem("l2_loaded"), 16)
                if runs(s, 4):
                    sp.wait_ge(sem("consts"), 16)
                    sp.wait_ge(sem("l3_out"), this[4])
                    if again[4]:
                        sp.wait_ge(sem("l3_stored"), 16 * past[4])
                    sp.dma_start(out_d[s - 4], y_out[par][:]).then_inc(sem("l3_stored"), 16)

            sweep(step_of, sp)
            sp.wait_ge(sem("l3_stored"), 16 * B)

        @block.tensor
        def _(pe):
            pe.wait_ge(sem("early_consts"), 16)

            def step_of(s, par):
                this, past, again = counts(s)
                on = [runs(s, g) for g in range(STAGES)]

                def claim(name, mine):
                    free = bank_free(s, name, mine)
                    if free:
                        pe.wait_ge(*free)

                def turn(dst, src):
                    for t in range(NT):
                        mm = pe.transpose(dst[:, t * P:(t + 1) * P], src[:, t, :], ident)
                    return mm

                def inputs01(a):
                    if a == 0:
                        pe.wait_ge(sem("l0_loaded"), 32 * this[0])
                    elif again[0]:
                        pe.wait_ge(sem("l0_x"), past[0])
                    if a == 1 and not again[1]:
                        pe.wait_ge(sem("setup_v"), 1)
                    claim("AD"[a], f"l{a}_xT_read")
                    turn((bA, bD)[a], (x0, x1)[a][par]).then_inc(sem(f"l{a}_xT_full"), 1)

                def project(a):
                    pe.wait_ge(sem(f"l{a}_xT_read"), this[a])
                    if a == 0 and not again[0]:
                        pe.wait_ge(sem("w_ext"), 1)
                    claim("F", f"l{a}_he_read")
                    W = P + 2 * HEADS
                    for t in range(NT):
                        mm = pe.matmul(bF[:, t * W:(t + 1) * W], xT01[:, a, t * P:(t + 1) * P], w_ext[a][:],
                                       start=True, stop=True)
                    mm.then_inc(sem(f"l{a}_he_full"), 1)

                def spread(a):
                    pe.wait_ge(sem(f"l{a}_he_read"), this[a])
                    for hp, (dst, name) in enumerate(((bF, "F"), (bG, "G"))):
                        claim(name, f"l{a}_max_p{hp}")
                        for h in range(2):
                            for t in range(NT):
                                at = P + HEADS + 2 * hp + h
                                mm = pe.transpose(dst[:, h * N + t * P:h * N + (t + 1) * P],
                                                  he[a][:, t, at:at + 1].broadcast_to([P, P]), ident)
                        mm.then_inc(sem(f"l{a}_spread_p{hp}"), 1)

                def turn_scores(a, k):
                    m, hp = CHUNKS[k]
                    dst, name = ((bD, "D"), (bE, "E"))[k % 2]
                    if a == 0:
                        pe.wait_ge(sem(f"l0_sc_p{hp}"), this[0])
                    elif again[1]:
                        pe.wait_ge(sem(f"l1_sc_p{hp}"), past[1])
                    claim(name, f"{TAIL[a]}_exp_c{k}")
                    for h in range(2):
                        for t in range(NT):
                            mm = pe.transpose(dst[:, h * N + t * P:h * N + (t + 1) * P],
                                              sc[a][:, t, 2 * hp + h, m * P:(m + 1) * P], ident)
                    mm.then_inc(sem(f"{TAIL[a]}_turned_c{k}"), 1)

                def aggregate(a):
                    pe.wait_ge(sem(f"{TAIL[a]}_exp_c3"), this[TSTAGE[a]])
                    claim("A", f"{TAIL[a]}_agg_read")
                    for part in range(2):
                        for m in range(NT):
                            for h in range(HEADS):
                                lhs = he[a][:, m, h * DH:(h + 1) * DH] if part == 0 else ones[:]
                                mm = pe.matmul(bA[h * DH:(h + 1) * DH, part * N:(part + 1) * N], lhs,
                                               pT[a][:, m, h, :], start=(m == 0), stop=(m == NT - 1),
                                               skip_group_check=True)
                    mm.then_inc(sem(f"{TAIL[a]}_agg_full"), 1)

                def back01(a):
                    pe.wait_ge(sem(f"{TAIL[a]}_agg_read"), this[TSTAGE[a]])
                    claim("A", f"{TAIL[a]}_o_read")
                    for k in range(2):
                        for t in range(NT):
                            mm = pe.transpose(bA[:, k * N + t * P:k * N + (t + 1) * P],
                                              aggT[a][:, k, t * P:(t + 1) * P], ident)
                    mm.then_inc(sem(f"{TAIL[a]}_o_full"), 1)

                def product(dst, name, column, moving, at, first, last):
                    column += OFFSET[name][0] - SPLIT
                    w_hi, w_lo = (w[:, column:column + P] for w in w_parts)
                    hi, lo = (m[:, at:at + N] for m in moving)
                    pe.matmul(dst, w_hi, lo, start=first, stop=False, skip_group_check=True)
                    pe.matmul(dst, w_lo, hi, start=False, stop=False, skip_group_check=True)
                    return pe.matmul(dst, w_hi, hi, start=False, stop=last, skip_group_check=True)

                def taps(k0, k1):
                    if k0 == 0:
                        if not again[3]:
                            pe.wait_ge(sem("w_lo"), 1)
                        if again[2]:
                            pe.wait_ge(sem("l2_h1_lo"), past[2])
                        claim("H", "l2t_conv2_read")
                    for k in range(k0, k1):
                        mm = product(bH[:, 0:N], "conv2", k * P, h1_parts, k, k == 0, k == TAPS - 1)
                    if k1 == TAPS:
                        mm.then_inc(sem("l2t_conv2_full"), 1)

                def gate(dst, g):
                    if g == 0:
                        pe.wait_ge(sem("l2t_xnmp_lo"), this[3])
                    product(dst, "wih", (3 + g) * P, xnmp_parts, 0, True, False)
                    if g < 2:
                        product(dst, "whh", g * P, x_parts[1 - par], 0, False, False)
                    if g == 0:
                        pe.wait_ge(sem("l2t_xconv_lo"), this[3])
                    return product(dst, "wih", g * P, xconv_parts, 0, False, True)

                if on[3]:
                    taps(0, 7)
                if on[0]:
                    inputs01(0)
                if on[3]:
                    taps(7, 9)
                    if again[2]:
                        pe.wait_ge(sem("l2_aT"), past[2])
                        pe.wait_ge(sem("l2_msg"), past[2])
                    claim("C", "l2t_xnmp_read")
                    for m in range(NT):
                        mm = pe.matmul(bC[:, 0:N], msg[:, m, :], aT[:, m, :], start=(m == 0), stop=(m == NT - 1))
                    mm.then_inc(sem("l2t_xnmp_full"), 1)
                    taps(9, 11)
                if on[0]:
                    project(0)
                if on[1]:
                    inputs01(1)
                if on[3]:
                    taps(11, 14)
                if on[2]:
                    turn_scores(1, 0)
                    turn_scores(1, 1)
                if on[0]:
                    spread(0)
                if on[2]:
                    turn_scores(1, 2)
                    turn_scores(1, 3)
                if on[3]:
                    taps(14, TAPS)
                if on[2]:
                    aggregate(1)
                if on[1]:
                    project(1)
                if on[4]:
                    pe.wait_ge(sem("l3_h"), this[4])
                    claim("B", "l3_hT_read")
                    turn(bB, h3).then_inc(sem("l3_hT_full"), 1)
                if on[2]:
                    back01(1)
                if on[3]:
                    claim("C", "l2t_rz_read")
                    gate(bC[:, 0:N], 0)
                    claim("H", "l2t_inhn_read")
                    gate(bH[:, 0:N], 2)
                    product(bH[:, N:2 * N], "whh", 2 * P, x_parts[1 - par], 0, True, True)\
                        .then_inc(sem("l2t_inhn_full"), 1)
                    gate(bC[:, N:2 * N], 1).then_inc(sem("l2t_rz_full"), 1)
                if on[4]:
                    claim("B", "l3_agg_read")
                    for m in range(NT):
                        mm = pe.matmul(bB[:, 0:N], h3[:, m, :], adjT[par][:, m, :],
                                       start=(m == 0), stop=(m == NT - 1))
                    mm.then_inc(sem("l3_agg_full"), 1)
                if on[0]:
                    turn_scores(0, 0)
                    turn_scores(0, 1)
                if on[2]:
                    pe.wait_ge(sem("l2_loaded"), 16 * this[2])
                    claim("B", "l2_adjT_read")
                    for m in range(NT):
                        for t in range(NT):
                            mm = pe.transpose(bB[:, m * N + t * P:m * N + (t + 1) * P],
                                              adj_b[par][:, t, m * P:(m + 1) * P], ident)
                    mm.then_inc(sem("l2_adjT_full"), 1)
                if on[1]:
                    spread(1)
                if on[0]:
                    turn_scores(0, 2)
                if on[2]:
                    pe.wait_ge(sem("l1t_x"), this[2])
                    claim("C", "l2_xT_read")
                    turn(bC, x2).then_inc(sem("l2_xT_full"), 1)
                if on[0]:
                    turn_scores(0, 3)
                if on[4]:
                    pe.wait_ge(sem("l3_agg_read"), this[4])
                    claim("B", "l3_conv_read")
                    for t in range(NT):
                        pe.matmul(bB[:, t * P:(t + 1) * P], agg3[:, t * P:(t + 1) * P], c("wrel"),
                                  start=True, stop=False)
                        mm = pe.matmul(bB[:, t * P:(t + 1) * P], h3T[:, t * P:(t + 1) * P], c("wroot"),
                                       start=False, stop=True)
                    mm.then_inc(sem("l3_conv_full"), 1)
                if on[2]:
                    pe.wait_ge(sem("l2_xT_read"), this[2])
                    claim("E", "l2_h1")
                    pe.matmul(bE[:, 0:N], c("conv1"), xT2[par][:], start=True, stop=True)
                    pe.matmul(bE[0:96, N:2 * N], c("wse"), xT2[par][:], start=True, stop=True)\
                        .then_inc(sem("l2_c1s_full"), 1)
                if on[0]:
                    aggregate(0)
                if on[2]:
                    pe.wait_ge(sem("l2_se"), this[2])
                    claim("D", "l2_near")
                    for t in range(NT):
                        mm = pe.matmul(bD[:, t * N:(t + 1) * N], seL[:, t * P:(t + 1) * P], seR[:],
                                       start=True, stop=True)
                    mm.then_inc(sem("l2_dist_full"), 1)
                if on[3]:
                    pe.wait_ge(sem("l2t_sum"), this[3])
                    claim("B", "l2t_back_read")
                    for t in range(NT):
                        mm = pe.transpose(bB[:, t * P:(t + 1) * P], yT2[:, t * P:(t + 1) * P], ident)
                    mm.then_inc(sem("l2t_back_full"), 1)
                if on[2]:
                    claim("C", "l2_msg_read")
                    for t in range(NT):
                        mm = pe.matmul(bC[:, t * P:(t + 1) * P], xT2[par][:, t * P:(t + 1) * P], c("wmsg"),
                                       start=True, stop=True)
                    mm.then_inc(sem("l2_msg_full"), 1)
                if on[0]:
                    back01(0)

            sweep(step_of, pe)

        @block.scalar
        def _(act):

            def step_of(s, par):
                this, past, again = counts(s)
                on = [runs(s, g) for g in range(STAGES)]

                def leaky(a, hp):
                    act.wait_ge(sem(f"l{a}_offsets"), this[a])
                    if again[a]:
                        act.wait_ge(sem(f"l{a}_sc_p{hp}"), past[a])
                    for t in range(NT):
                        for h in (2 * hp, 2 * hp + 1):
                            last = act.activation(low[a][:, t, h, :], sc[a][:, t, h, :], ACT.Identity,
                                                  bias=off2[a][:, t, h:h + 1], scale=SLOPE)
                    last.then_inc(sem(f"l{a}_leaky_p{hp}"), 1)

                def exps(a, k):
                    m, hp = CHUNKS[k]
                    g = TSTAGE[a]
                    act.wait_ge(sem(f"{TAIL[a]}_turned_c{k}"), this[g])
                    if k == 0:
                        if again[g]:
                            act.wait_ge(sem(f"{TAIL[a]}_agg_full"), past[g])
                    src = (bD, bE)[k % 2]
                    act.activation(pT[a][:, m, 2 * hp:2 * hp + 2, :], src[:].rearrange("p (h n) -> p h n", h=2),
                                   ACT.Exp).then_inc(sem(f"{TAIL[a]}_exp_c{k}"), 1)

                def sums_out(a):
                    g = TSTAGE[a]
                    act.wait_ge(sem(f"{TAIL[a]}_agg_full"), this[g])
                    if again[g]:
                        act.wait_ge(sem(f"{TAIL[a]}_o_full"), past[g])
                    act.activation(aggT[a][:], bA[:].rearrange("p (k n) -> p k n", k=2), ACT.Copy)\
                        .then_inc(sem(f"{TAIL[a]}_agg_read"), 1)

                def inputs01(a):
                    act.wait_ge(sem(f"l{a}_xT_full"), this[a])
                    if a == 1 and not again[1]:
                        act.wait_ge(sem("setup_v"), 1)
                    if again[a]:
                        act.wait_ge(sem(f"l{a}_he_full"), past[a])
                    act.activation(xT01[:, a, :], (bA, bD)[a][:, 0:N], ACT.Copy).then_inc(sem(f"l{a}_xT_read"), 1)

                def he_copy(a):
                    act.wait_ge(sem(f"l{a}_he_full"), this[a])
                    if a == 0 and again[0]:
                        act.wait_ge(sem("l0_agg_full"), past[0])
                    if a == 1 and on[2]:
                        act.wait_ge(sem("l1t_agg_full"), this[2])
                    if again[a]:
                        act.wait_ge(sem(f"l{a}_offsets"), past[a])
                    W = P + 2 * HEADS
                    act.activation(he[a][:], bF[:, 0:NT * W].rearrange("p (t w) -> p t w", t=NT), ACT.Copy)\
                        .then_inc(sem(f"l{a}_he_read"), 1)

                if on[0]:
                    inputs01(0)
                if on[3]:
                    act.wait_ge(sem("l2t_xnmp_full"), this[3])
                    if again[3]:
                        act.wait_ge(sem("l2t_inhn_full"), past[3])
                    act.activation(xnmp[:], bC[:, 0:N], ACT.Copy).then_inc(sem("l2t_xnmp_read"), 1)
                if on[0]:
                    he_copy(0)
                if on[1]:
                    inputs01(1)
                if on[3]:
                    act.wait_ge(sem("l2t_xnmp_read"), this[3])
                    act.activation(xnmp_parts[0][:], xnmp[:], ACT.Copy).then_inc(sem("l2t_xnmp_hi"), 1)
                if on[2]:
                    exps(1, 0)
                    exps(1, 1)
                    exps(1, 2)
                    exps(1, 3)
                if on[3]:
                    act.wait_ge(sem("l2t_conv2_read"), this[3])
                    if again[3]:
                        act.wait_ge(sem("l2t_xconv_lo"), past[3])
                    act.activation(xconv[:], conv[:], ACT.Relu, bias=bn_b[:, 1:2]).then_inc(sem("l2t_xconv"), 1)
                    act.wait_ge(sem("l2t_xconv"), this[3])
                    if again[3]:
                        act.wait_ge(sem("l2t_inhn_full"), past[3])
                    act.activation(xconv_parts[0][:], xconv[:], ACT.Copy).then_inc(sem("l2t_xconv_hi"), 1)
                if on[2]:
                    sums_out(1)
                if on[1]:
                    he_copy(1)
                if on[0]:
                    leaky(0, 0)
                if on[4]:
                    act.wait_ge(sem("l3_hT_full"), this[4])
                    if again[4]:
                        act.wait_ge(sem("l3_conv_full"), past[4])
                    act.activation(h3T[:], bB[:, 0:N], ACT.Copy).then_inc(sem("l3_hT_read"), 1)
                if on[0]:
                    leaky(0, 1)
                if on[3]:
                    act.wait_ge(sem("l2t_inhn_full"), this[3])
                    if again[3]:
                        act.wait_ge(sem("l2t_q"), past[3])
                    act.activation(hb[:], bH[:, N:2 * N], ACT.Identity, bias=bhnh[:, 0:1], scale=0.5)\
                        .then_inc(sem("l2t_hb"), 1)
                    act.wait_ge(sem("l2t_rz_full"), this[3])
                    act.activation(tr[:], bC[:, 0:N], ACT.Tanh, bias=brzh[:, 0:1], scale=0.5)\
                        .then_inc(sem("l2t_tr"), 1)
                if on[4]:
                    act.wait_ge(sem("l3_agg_full"), this[4])
                    act.activation(agg3[:], bB[:, 0:N], ACT.Copy).then_inc(sem("l3_agg_read"), 1)
                if on[0]:
                    exps(0, 0)
                if on[3]:
                    act.activation(tz[:], bC[:, N:2 * N], ACT.Tanh, bias=brzh[:, 1:2], scale=0.5)\
                        .then_inc(sem("l2t_rz_read"), 1)
                if on[2]:
                    act.wait_ge(sem("l2_adjT_full"), this[2])
                    if on[4]:
                        act.wait_ge(sem("l3_agg_full"), this[4])
                    act.activation(adjT[par][:], bB[:].rearrange("p (t n) -> p t n", t=NT), ACT.Copy)\
                        .then_inc(sem("l2_adjT_read"), 1)
                if on[0]:
                    exps(0, 1)
                    exps(0, 2)
                if on[2]:
                    act.wait_ge(sem("l2_xT_full"), this[2])
                    if again[3]:
                        act.wait_ge(sem("l2t_inhn_full"), past[3])
                        act.wait_ge(sem("l2t_blend"), past[3])
                        act.wait_ge(sem("l2t_sum"), past[3])
                    act.activation(xT2[par][:], bC[:, 0:N], ACT.Copy).then_inc(sem("l2_xT_read"), 1)
                if on[0]:
                    exps(0, 3)
                if on[3]:
                    act.wait_ge(sem("l2t_inhn_read"), this[3])
                    act.activation(nn[:], pn[:], ACT.Tanh, bias=c("bih", 2, 3)).then_inc(sem("l2t_nn"), 1)
                if on[2]:
                    act.wait_ge(sem("l2_xT_read"), this[2])
                    act.activation(x_parts[par][0][:], xT2[par][:], ACT.Copy).then_inc(sem("l2_xT_hi"), 1)
                    act.wait_ge(sem("l2_c1s_full"), this[2])
                    if on[3]:
                        act.wait_ge(sem("l2t_conv2_full"), this[3])
                    if again[2]:
                        act.wait_ge(sem("l2_dist_full"), past[2])
                        act.wait_ge(sem("l2_h1_lo"), past[2])
                    act.activation(seL[0:3, :], bE[0:3, N:2 * N], ACT.Identity, bias=bse2[0:3, :], scale=2.0)
                    act.activation(seR[0:3, :], bE[0:3, N:2 * N], ACT.Identity, bias=c("bse")[0:3, :])
                    act.activation(seL[32:35, :], bE[32:35, N:2 * N], ACT.Square, bias=c("bse")[32:35, :])
                    act.activation(seR[64:67, :], bE[64:67, N:2 * N], ACT.Square, bias=c("bse")[64:67, :])\
                        .then_inc(sem("l2_se"), 1)
                    act.activation(h1[:, PAD:PAD + N], bE[:, 0:N], ACT.Relu, bias=bn_b[:, 0:1],
                                   scale=bn_s[:, 0:1]).then_inc(sem("l2_h1"), 1)
                    act.wait_ge(sem("l2_h1"), this[2])
                    act.activation(h1_parts[0][:], h1[:], ACT.Copy).then_inc(sem("l2_h1_hi"), 1)
                if on[0]:
                    sums_out(0)
                if on[3]:
                    act.wait_ge(sem("l2t_back_full"), this[3])
                    if again[3]:
                        act.wait_ge(sem("l2t_x"), past[3])
                    act.activation(y[2][:], bB[:, 0:NT * D].rearrange("p (t d) -> p t d", t=NT), ACT.Copy)\
                        .then_inc(sem("l2t_back_read"), 1)
                if on[2]:
                    act.wait_ge(sem("l2_dist_full"), this[2])
                    if again[2]:
                        act.wait_ge(sem("l2_aT"), past[2])
                    act.activation(near[:], bD[:].rearrange("p (t n) -> p t n", t=NT), ACT.Exp)\
                        .then_inc(sem("l2_near"), 1)
                if on[1]:
                    leaky(1, 0)
                if on[2]:
                    act.wait_ge(sem("l2_msg_read"), this[2])
                    if on[3]:
                        act.wait_ge(sem("l2t_xnmp_full"), this[3])
                    act.activation(msg[:], msg_b[:], ACT.Relu).then_inc(sem("l2_msg"), 1)
                if on[1]:
                    leaky(1, 1)

            sweep(step_of, act)

        @block.gpsimd
        def _(gp):
            nc.gpsimd.memset(eps[:], EPS)
            nc.gpsimd.memset(mhalf[:], -0.5).then_inc(sem("mhalf"), 1)
            gp.wait_ge(sem("mhalf"), 1)
            gp.wait_ge(sem("bn_v"), 1)
            gp.tensor_tensor(bn_r[:], bn_v[:], mhalf[:], ALU.pow).then_inc(sem("bn_r"), 1)

            gp.wait_ge(sem("late_consts"), 16)
            gp.tensor_copy(w_parts[0][:], cst[:, SPLIT:WIDTH]).then_inc(sem("w_hi"), 1)
            gp.wait_ge(sem("w_hi"), 1)
            gp.tensor_tensor(w_parts[1][:], cst[:, SPLIT:WIDTH], w_parts[0][:].bitcast(F32), ALU.subtract)\
                .then_inc(sem("w_lo"), 1)

            def rsqrt(k, what, count):
                gp.wait_ge(sem(f"{what}stats"), count)
                gp.tensor_tensor(ve[k][:], mv[k][:, :, 1], eps[:], ALU.add).then_inc(sem(f"{what}ve"), 1)
                gp.wait_ge(sem(f"{what}ve"), count)
                gp.tensor_tensor(rstd[k][:], ve[k][:], mhalf[:], ALU.pow).then_inc(sem(f"{what}rstd"), 1)

            def step_of(s, par):
                this, past, again = counts(s)
                on = [runs(s, g) for g in range(STAGES)]

                if on[4]:
                    rsqrt(4, "l3_in_", this[4])
                if on[3]:
                    gp.wait_ge(sem("l2t_xnmp_hi"), this[3])
                    if again[3]:
                        gp.wait_ge(sem("l2t_inhn_full"), past[3])
                    gp.tensor_tensor(xnmp_parts[1][:], xnmp[:], xnmp_parts[0][:].bitcast(F32), ALU.subtract)\
                        .then_inc(sem("l2t_xnmp_lo"), 1)
                if on[4]:
                    gp.wait_ge(sem("l3_hn"), this[4])
                    gp.tensor_tensor(hg[:], hn[:], c("gamma").unsqueeze(1).broadcast_to([P, NT, D]), ALU.mult)\
                        .then_inc(sem("l3_hg"), 1)
                    gp.wait_ge(sem("l3_hg"), this[4])
                    if again[4]:
                        gp.wait_ge(sem("l3_agg_full"), past[4])
                    gp.tensor_tensor(h3[:], hg[:], c("beta").unsqueeze(1).broadcast_to([P, NT, D]), ALU.add)\
                        .then_inc(sem("l3_h"), 1)
                if on[2]:
                    if again[2]:
                        gp.wait_ge(sem("l1t_biased"), past[2])
                    gp.wait_ge(sem("l0_x"), this[2])
                    gp.tensor_tensor(xb1[:], x1[1 - par][:], c("bias1").unsqueeze(1).broadcast_to([P, NT, D]),
                                     ALU.add).then_inc(sem("l1t_xb"), 1)
                if on[3]:
                    gp.wait_ge(sem("l2t_xconv_hi"), this[3])
                    if again[3]:
                        gp.wait_ge(sem("l2t_inhn_full"), past[3])
                    gp.tensor_tensor(xconv_parts[1][:], xconv[:], xconv_parts[0][:].bitcast(F32), ALU.subtract)\
                        .then_inc(sem("l2t_xconv_lo"), 1)
                if on[4]:
                    gp.wait_ge(sem("l2t_x"), this[4])
                    if again[4]:
                        gp.wait_ge(sem("l3_y"), past[4])
                    gp.tensor_tensor(x2x[:], x3[par][:], x3[par][:], ALU.add).then_inc(sem("l3_x2x"), 1)
                if on[2]:
                    gp.wait_ge(sem("l1t_leaky"), this[2])
                    if again[2]:
                        gp.wait_ge(sem("l1t_x"), past[2])
                    gp.tensor_tensor(y[1][:], y1b[:], x1[1 - par][:], ALU.add).then_inc(sem("l1t_sum"), 1)
                    rsqrt(1, "l1t_", this[2])
                if on[3]:
                    gp.wait_ge(sem("l2t_nn"), this[3])
                    if again[3]:
                        gp.wait_ge(sem("l2t_blend"), past[3])
                    gp.tensor_tensor(dl[:], xT2[1 - par][:], nn[:], ALU.subtract).then_inc(sem("l2t_dl"), 1)
                    gp.wait_ge(sem("l2t_o2"), this[3])
                    if again[3]:
                        gp.wait_ge(sem("l2t_back_full"), past[3])
                    gp.tensor_tensor(yT2[:], o2[:], xT2[1 - par][:], ALU.add).then_inc(sem("l2t_sum"), 1)
                if on[2]:
                    gp.wait_ge(sem("l2_h1_hi"), this[2])
                    if on[3]:
                        gp.wait_ge(sem("l2t_conv2_full"), this[3])
                    gp.tensor_tensor(h1_parts[1][:], h1[:], h1_parts[0][:].bitcast(F32), ALU.subtract)\
                        .then_inc(sem("l2_h1_lo"), 1)
                    gp.wait_ge(sem("l2_xT_hi"), this[2])
                    if again[3]:
                        gp.wait_ge(sem("l2t_inhn_full"), past[3])
                    gp.tensor_tensor(x_parts[par][1][:], xT2[par][:], x_parts[par][0][:].bitcast(F32), ALU.subtract)\
                        .then_inc(sem("l2_xT_lo"), 1)
                if on[0]:
                    gp.wait_ge(sem("l0_o_read"), this[0])
                    if again[0]:
                        gp.wait_ge(sem("l0_x"), past[0])
                    gp.tensor_tensor(y[0][:], att[0][:], x0[par][:], ALU.add).then_inc(sem("l0_sum"), 1)
                if on[4]:
                    rsqrt(3, "l3_", this[4])
                if on[0]:
                    rsqrt(0, "l0_", this[0])
                if on[3]:
                    rsqrt(2, "l2t_", this[3])

            sweep(step_of, gp)

        @block.vector
        def _(dve):
            dve.wait_ge(sem("early_consts"), 16)
            links = [0]

            def link(ins):
                links[0] += 1
                ins.then_inc(sem("setup_chain"), 1)
                dve.wait_ge(sem("setup_chain"), links[0])

            for a in range(2):
                dve.tensor_copy(w_ext[a][:, 0:P], c(f"w{a}"))
                for r, side in enumerate("lr"):
                    last = dve.tensor_tensor(prod[:, 2 * a + r, :], c(f"w{a}"), c(f"a{a}{side}"), ALU.mult)
                link(last)
                last = dve.tensor_reduce(w_ext[a][:, P:P + 2 * HEADS],
                                         prod[:, 2 * a:2 * a + 2, :].rearrange("p r (h d) -> p (r h) d", d=DH),
                                         AX.X, ALU.add)
                if a == 0:
                    last.then_inc(sem("w_ext"), 1)
            dve.memset(ones[:], 1.0)
            dve.memset(h1[:], 0.0)
            dve.memset(seL[:], 0.0)
            link(dve.memset(seR[:], 0.0))
            dve.memset(seL[64:67, :], -1.0)
            dve.memset(seR[32:35, :], -1.0)
            dve.wait_ge(sem("consts"), 16)
            for k, base in enumerate(("bn1", "bn2")):
                last = dve.tensor_scalar(bn_v[:, k:k + 1], c(base, 3, 4), EPS, None, ALU.add)
            last.then_inc(sem("bn_v"), 1)
            dve.tensor_scalar(bse2[:], c("bse"), 2.0, None, ALU.mult)
            dve.tensor_scalar(bhnh[:], c("bhh", 2, 3), 0.5, None, ALU.mult)
            link(dve.tensor_tensor(brz[:], c("bih", 0, 2), c("bhh", 0, 2), ALU.add))
            dve.tensor_scalar(brzh[:], brz[:], 0.5, None, ALU.mult)
            dve.wait_ge(sem("bn_r"), 1)
            for k, base in enumerate(("bn1", "bn2")):
                last = dve.tensor_tensor(bn_s[:, k:k + 1], c(base, 0, 1), bn_r[:, k:k + 1], ALU.mult)
            link(last)
            for k, base in enumerate(("bn1", "bn2")):
                last = dve.tensor_tensor(bn_ms[:, k:k + 1], c(base, 2, 3), bn_s[:, k:k + 1], ALU.mult)
            link(last)
            for k, base in enumerate(("bn1", "bn2")):
                last = dve.tensor_tensor(bn_b[:, k:k + 1], c(base, 1, 2), bn_ms[:, k:k + 1], ALU.subtract)
            last.then_inc(sem("setup_v"), 1)

            def step_of(s, par):
                this, past, again = counts(s)
                on = [runs(s, g) for g in range(STAGES)]

                def moments(k, what, src):
                    for t in range(NT):
                        last = dve.bn_stats(st[k][:, t, :], src(t))
                    last.then_inc(sem(f"{what}bn"), 1)

                def stats(k, what, count):
                    dve.wait_ge(sem("consts"), 16)
                    dve.wait_ge(sem(f"{what}bn"), count)
                    for t in range(NT):
                        last = dve.bn_aggr(mv[k][:, t, :], st[k][:, t, :])
                    last.then_inc(sem(f"{what}stats"), 1)

                def normalise(k, what, count, src, dst, done):
                    dve.wait_ge(sem(f"{what}rstd"), count)
                    for t in range(NT):
                        last = dve.tensor_scalar(dst[:, t, :], src(t), mv[k][:, t, 0:1], rstd[k][:, t:t + 1],
                                                 ALU.subtract, ALU.mult)
                    last.then_inc(sem(done), 1)

                def maxima(a, hp):
                    edge = edge0 if a == 0 else edge1[1 - par]
                    dve.wait_ge(sem("consts"), 16)
                    dve.wait_ge(sem(f"l{a}_spread_p{hp}"), this[a])
                    if a == 0:
                        dve.wait_ge(sem("l0_edge0"), this[0])
                    src = (bF, bG)[hp]
                    for t in range(NT):
                        for h in range(2):
                            last = dve.tensor_tensor_reduce(
                                out=sc[a][:, t, 2 * hp + h, :], in0=edge[:, t, :], in1=src[:, h * N:(h + 1) * N],
                                scale=1.0, scalar=-3.0e38, op0=ALU.add, op1=ALU.max,
                                accum_out=rmax[a][:, t, 2 * hp + h:2 * hp + h + 1])
                    last.then_inc(sem(f"l{a}_max_p{hp}"), 1)

                def peak(a):
                    left = he[a][:, :, P:P + HEADS]
                    dve.wait_ge(sem(f"l{a}_max_p1"), this[a])
                    dve.tensor_tensor(pre[a][:], rmax[a][:], left, ALU.add).then_inc(sem(f"l{a}_pre"), 1)

                def row_maximum(a):
                    dve.wait_ge(sem(f"l{a}_pre"), this[a])
                    dve.scalar_tensor_tensor(mrow[a][:], pre[a][:], SLOPE, pre[a][:], ALU.mult, ALU.max)\
                        .then_inc(sem(f"l{a}_mrow"), 1)

                def offsets(a):
                    left = he[a][:, :, P:P + HEADS]
                    dve.wait_ge(sem(f"l{a}_mrow"), this[a])
                    if again[a]:
                        dve.wait_ge(sem(f"l{a}_leaky_p1"), past[a])
                    dve.tensor_tensor(off1[a][:], left, mrow[a][:], ALU.subtract)
                    dve.scalar_tensor_tensor(off2[a][:], left, SLOPE, mrow[a][:], ALU.mult, ALU.subtract)\
                        .then_inc(sem(f"l{a}_offsets"), 1)

                def shift(a, hp):
                    dve.wait_ge(sem(f"l{a}_leaky_p{hp}"), this[a])
                    dve.wait_ge(sem(f"l{a}_offsets"), this[a])
                    for t in range(NT):
                        for h in (2 * hp, 2 * hp + 1):
                            last = dve.scalar_tensor_tensor(sc[a][:, t, h, :], sc[a][:, t, h, :], off1[a][:, t, h:h + 1],
                                                            low[a][:, t, h, :], ALU.add, ALU.max)
                    last.then_inc(sem(f"l{a}_sc_p{hp}"), 1)

                def invert(a):
                    g = TSTAGE[a]
                    dve.wait_ge(sem(f"{TAIL[a]}_o_full"), this[g])
                    sums = bA[:, N:2 * N].rearrange("p (t h d) -> p t h d", t=NT, d=DH)
                    dve.reciprocal(rden[a][:], sums[:, :, :, 0]).then_inc(sem(f"{TAIL[a]}_rden"), 1)

                def divide(a):
                    g = TSTAGE[a]
                    if again[g]:
                        dve.wait_ge(sem(("l0_sum", "l1t_biased")[a]), past[g])
                    dve.wait_ge(sem(f"{TAIL[a]}_rden"), this[g])
                    dve.tensor_tensor(att[a][:].rearrange("p t (h d) -> p t h d", d=DH),
                                      bA[:, 0:N].rearrange("p (t h d) -> p t h d", t=NT, d=DH),
                                      rden[a][:].unsqueeze(3).broadcast_to([P, NT, HEADS, DH]), ALU.mult)\
                        .then_inc(sem(f"{TAIL[a]}_o_read"), 1)

                def tiles(t2):
                    return t2[:, 0:NT * D].rearrange("p (t d) -> p t d", t=NT)

                if on[4]:
                    if again[3]:
                        dve.wait_ge(sem("l2t_x"), past[3])
                    moments(4, "l3_in_", lambda t: x3[par][:, t, :])
                if on[0]:
                    dve.wait_ge(sem("l0_loaded"), 32 * this[0])
                    dve.tensor_scalar(edge0[:], adj_a[par][:], 0.0, NEG, ALU.is_le, ALU.mult)\
                        .then_inc(sem("l0_edge0"), 1)
                if on[4]:
                    stats(4, "l3_in_", this[4])
                if on[0]:
                    maxima(0, 0)
                if on[4]:
                    if again[4]:
                        dve.wait_ge(sem("l3_h"), past[4])
                    normalise(4, "l3_in_", this[4], lambda t: x3[par][:, t, :], hn, "l3_hn")
                if on[3]:
                    dve.wait_ge(sem("l2t_conv2_full"), this[3])
                    dve.scalar_tensor_tensor(conv[:], bH[:, 0:N], bn_s[:, 1:2], xT2[1 - par][:], ALU.mult, ALU.add)\
                        .then_inc(sem("l2t_conv2_read"), 1)
                if on[0]:
                    maxima(0, 1)
                    peak(0)
                    row_maximum(0)
                    offsets(0)
                    dve.wait_ge(sem("l0_loaded"), 32 * this[0])
                    dve.tensor_scalar(padmask[:], adj_a[par][:], EPS, NEG, ALU.is_le, ALU.mult)\
                        .then_inc(sem("l0_pad"), 1)
                if on[2]:
                    invert(1)
                    divide(1)
                    dve.wait_ge(sem("l1t_o_read"), this[2])
                    dve.wait_ge(sem("l1t_xb"), this[2])
                    dve.tensor_tensor(y1a[:], att[1][:], xb1[:], ALU.add).then_inc(sem("l1t_biased"), 1)
                    dve.wait_ge(sem("l1t_biased"), this[2])
                    if again[2]:
                        dve.wait_ge(sem("l1t_sum"), past[2])
                    dve.scalar_tensor_tensor(y1b[:], y1a[:], 0.5, y1a[:], ALU.mult, ALU.max).then_inc(sem("l1t_leaky"), 1)
                if on[0]:
                    shift(0, 0)
                if on[2]:
                    dve.wait_ge(sem("l1t_sum"), this[2])
                    moments(1, "l1t_", lambda t: y[1][:, t, :])
                    stats(1, "l1t_", this[2])
                if on[0]:
                    shift(0, 1)
                if on[2]:
                    if again[2]:
                        dve.wait_ge(sem("l2_xT_full"), past[2])
                    normalise(1, "l1t_", this[2], lambda t: y[1][:, t, :], x2, "l1t_x")
                if on[3]:
                    dve.wait_ge(sem("l2t_hb"), this[3])
                    dve.wait_ge(sem("l2t_tr"), this[3])
                    dve.scalar_tensor_tensor(q[:], tr[:], 1.0, hb[:], ALU.add, ALU.mult).then_inc(sem("l2t_q"), 1)
                    dve.wait_ge(sem("l2t_q"), this[3])
                    dve.tensor_tensor(pn[:], bH[:, 0:N], q[:], ALU.add).then_inc(sem("l2t_inhn_read"), 1)
                if on[1]:
                    maxima(1, 0)
                    maxima(1, 1)
                if on[3]:
                    dve.wait_ge(sem("l2t_rz_read"), this[3])
                    dve.wait_ge(sem("l2t_dl"), this[3])
                    dve.scalar_tensor_tensor(tzd[:], tz[:], 1.0, dl[:], ALU.add, ALU.mult)\
                        .then_inc(sem("l2t_blend"), 1)
                if on[1]:
                    peak(1)
                if on[3]:
                    dve.wait_ge(sem("l2t_blend"), this[3])
                    if again[3]:
                        dve.wait_ge(sem("l2t_sum"), past[3])
                    dve.scalar_tensor_tensor(o2[:], tzd[:], 0.5, nn[:], ALU.mult, ALU.add)\
                        .then_inc(sem("l2t_o2"), 1)
                if on[0]:
                    dve.wait_ge(sem("l0_pad"), this[0])
                    dve.scalar_tensor_tensor(edge1[par][:], adj_a[par][:], c("we"), padmask[:], ALU.mult, ALU.add)\
                        .then_inc(sem("l0_edge1"), 1)
                if on[4]:
                    dve.wait_ge(sem("l3_conv_full"), this[4])
                    dve.tensor_tensor(cb[:], tiles(bB), c("brel").unsqueeze(1).broadcast_to([P, NT, D]), ALU.add)\
                        .then_inc(sem("l3_conv_read"), 1)
                if on[1]:
                    row_maximum(1)
                if on[4]:
                    dve.wait_ge(sem("l3_conv_read"), this[4])
                    dve.wait_ge(sem("l3_x2x"), this[4])
                    dve.scalar_tensor_tensor(y[3][:], cb[:], 0.0, x2x[:], ALU.max, ALU.add)\
                        .then_inc(sem("l3_y"), 1)
                if on[1]:
                    offsets(1)
                if on[4]:
                    dve.wait_ge(sem("l3_y"), this[4])
                    moments(3, "l3_", lambda t: y[3][:, t, :])
                if on[2]:
                    dve.wait_ge(sem("l2_msg_full"), this[2])
                    if again[2]:
                        dve.wait_ge(sem("l2_msg"), past[2])
                    dve.tensor_tensor(msg_b[:], tiles(bC), c("bmsg").unsqueeze(1).broadcast_to([P, NT, D]), ALU.add)\
                        .then_inc(sem("l2_msg_read"), 1)
                if on[0]:
                    invert(0)
                if on[4]:
                    stats(3, "l3_", this[4])
                if on[0]:
                    divide(0)
                if on[3]:
                    dve.wait_ge(sem("l2t_back_read"), this[3])
                    moments(2, "l2t_", lambda t: y[2][:, t, :])
                if on[2]:
                    dve.wait_ge(sem("l2_near"), this[2])
                    dve.wait_ge(sem("l2_adjT_read"), this[2])
                    if on[3]:
                        dve.wait_ge(sem("l2t_xnmp_full"), this[3])
                    dve.tensor_tensor(aT[:], near[:], adjT[par][:], ALU.mult).then_inc(sem("l2_aT"), 1)
                if on[0]:
                    dve.wait_ge(sem("l0_sum"), this[0])
                    moments(0, "l0_", lambda t: y[0][:, t, :])
                    stats(0, "l0_", this[0])
                if on[1]:
                    shift(1, 0)
                if on[0]:
                    if again[1]:
                        dve.wait_ge(sem("l1_xT_full"), past[1])
                    normalise(0, "l0_", this[0], lambda t: y[0][:, t, :], x1[1 - par], "l0_x")
                if on[3]:
                    stats(2, "l2t_", this[3])
                if on[1]:
                    shift(1, 1)
                if on[4]:
                    if again[4]:
                        dve.wait_ge(sem("l3_stored"), 16 * past[4])
                    normalise(3, "l3_", this[4], lambda t: y[3][:, t, :], y_out[par], "l3_out")
                if on[3]:
                    if again[4]:
                        dve.wait_ge(sem("l3_x2x"), past[4])
                    normalise(2, "l2t_", this[3], lambda t: y[2][:, t, :], x3[1 - par], "l2t_x")

            sweep(step_of, dve)


def pack(v):
    def rows(a):
        return np.broadcast_to(np.reshape(a, (1, P)), (P, P))

    def cols(a):
        return np.reshape(a, (-1, P)).T

    wse, bse = np.zeros((P, 96), np.float32), np.zeros((P, 1), np.float32)
    for at in (0, 32, 64):
        wse[:, at:at + 3] = v["L2_gnn_w_se"].T
        bse[at:at + 3, 0] = v["L2_gnn_b_se"]
    a0, a1 = v["L0_gnn_a"], v["L1_gnn_a_w"][0]
    wih = v["L2_gnn_w_ih"]
    parts = {
        "ident": np.eye(P, dtype=np.float32),
        "w0": v["L0_gnn_W"], "w1": v["L1_gnn_W_proj"].T,
        "a0l": rows(a0[:, :DH]), "a0r": rows(a0[:, DH:]),
        "a1l": rows(np.tile(a1[:DH], HEADS)), "a1r": rows(np.tile(a1[DH:2 * DH], HEADS)),
        "bias1": rows(v["L1_gnn_bias"]),
        "conv1": v["L2_gnn_conv1_w"][:, :, 0].T,
        "conv2": v["L2_gnn_conv2_w"].transpose(1, 2, 0).reshape(P, TAPS * P),
        "wmsg": v["L2_gnn_w_msg"].T, "bmsg": rows(v["L2_gnn_b_msg"]), "wse": wse,
        "wih": np.concatenate([wih[:, :P].T, wih[:, P:].T], axis=1), "whh": v["L2_gnn_w_hh"].T,
        "wrel": v["L3_gnn_W_rel"], "wroot": v["L3_gnn_W_root"], "brel": rows(v["L3_gnn_b_rel"]),
        "gamma": rows(v["L3_gnn_ln_gamma"]), "beta": rows(v["L3_gnn_ln_beta"]),
        "bn1": np.stack([v[f"L2_gnn_bn1_{k}"] for k in "gbmv"], axis=1),
        "bn2": np.stack([v[f"L2_gnn_bn2_{k}"] for k in "gbmv"], axis=1),
        "bih": cols(v["L2_gnn_b_ih"]), "bhh": cols(v["L2_gnn_b_hh"]),
        "bse": bse, "we": np.broadcast_to(np.reshape(a1[2 * DH:], (1, 1)), (P, 1)),
    }
    return np.concatenate([parts[name] for name, _ in COLUMNS], axis=1)


def kernel(**inputs):
    import concourse.bacc as bacc
    from concourse.bass_utils import run_bass_kernel_spmd

    v = {name: np.asarray(a) for name, a in inputs.items()}
    arrays = {"in_x": np.ascontiguousarray(v["x"]), "in_adj": np.ascontiguousarray(v["adj"]),
              "in_consts": np.ascontiguousarray(pack(v))}
    nc = bacc.Bacc("TRN2", target_bir_lowering=False, num_devices=1)
    aps = [nc.dram_tensor(name, a.shape, F32, kind="ExternalInput").ap() for name, a in arrays.items()]
    out = nc.dram_tensor("out", v["x"].shape, F32, kind="ExternalOutput").ap()
    build(nc, *aps, out)
    r = run_bass_kernel_spmd(nc, [arrays], core_ids=[0])
    return r.results[0]["out"]
```
